# Optimizing a Trainium2 kernel written in Bass

```python
import numpy as np
import jax
import jax.numpy as jnp

def _softmax(x, axis=-1):
    return jax.nn.softmax(x, axis=axis)

def _gelu(x):
    return jax.nn.gelu(x, approximate=True)

def _silu(x):
    return jax.nn.silu(x)

def _sigmoid(x):
    return jax.nn.sigmoid(x)

def _layernorm(x, axis=-1, eps=1e-05):
    m = jnp.mean(x, axis=axis, keepdims=True)
    v = jnp.var(x, axis=axis, keepdims=True)
    return (x - m) / jnp.sqrt(v + eps)

def _scatter_add(tgt, idx, src, axis=0):
    return tgt.at[idx].add(src)

def _segment_sum(src, seg, n):
    return jax.ops.segment_sum(src, seg, n)
kernel_name = 'mk_prb_d2_jaxref_r8_25bf72'

def setup_inputs(seed: int=0):
    np.random.seed(seed)
    _w = jnp.asarray

    def _L0_attn_setup():
        import jax, jax.numpy as jnp
        import numpy as np
        DEPTH, DIM, DFF, VOCAB = (4, 64, 256, 512)
        EPS = 1e-05

        def layernorm(x, w, b):
            mu = jnp.mean(x, axis=-1, keepdims=True)
            var = jnp.mean((x - mu) ** 2, axis=-1, keepdims=True)
            return (x - mu) * jax.lax.rsqrt(var + EPS) * w + b

        def sconv(x, phazor_c, last_conv_c):
            B, L, D = x.shape
            r = jnp.abs(phazor_c)
            p = jnp.tanh(r) * jnp.exp(1j * jnp.angle(phazor_c))
            prog = p[None, :] ** jnp.arange(L, dtype=jnp.float32)[:, None]
            filt_fft = jnp.fft.fft(prog, n=2 * L, axis=0)
            x_fft = jnp.fft.fft(x.astype(jnp.complex64), n=2 * L, axis=1)
            conv = jnp.fft.ifft(filt_fft[None] * x_fft, axis=1)[:, :L]
            conv = conv + last_conv_c[None, None, :] * prog[None] * p[None, None, :]
            return conv.real.astype(x.dtype)

        def _forward(x, Win, bin, ln1_w, ln1_b, phz_re, phz_im, lc_re, lc_im, sc_lin, ln2_w, ln2_b, W1, b1, W2, b2, lnl_w, lnl_b, Wout, bout):
            h = jnp.einsum('blv,dv->bld', x, Win) + bin

            def body(h, p):
                l1w, l1b, pr, pi, lr, li, scl, l2w, l2b, w1, b1_, w2, b2_ = p
                y = jax.nn.silu(layernorm(h, l1w, l1b))
                y = sconv(y, pr + 1j * pi, lr + 1j * li)
                h = h + y * scl
                y = layernorm(h, l2w, l2b)
                y = jax.nn.silu(jnp.einsum('bld,fd->blf', y, w1) + b1_)
                y = jnp.einsum('blf,df->bld', y, w2) + b2_
                return (h + y, None)
            xs = (ln1_w, ln1_b, phz_re, phz_im, lc_re, lc_im, sc_lin, ln2_w, ln2_b, W1, b1, W2, b2)
            h, _ = jax.lax.scan(body, h, xs)
            h = layernorm(h, lnl_w, lnl_b)
            return jnp.einsum('bld,vd->blv', h, Wout) + bout
        key = jax.random.key(seed)
        ks = jax.random.split(key, 20)
        f32 = jnp.float32
        inp = {}
        inp['x'] = jax.random.normal(ks[0], (2, 512, VOCAB), dtype=f32)
        inp['Win'] = jax.random.normal(ks[1], (DIM, VOCAB), dtype=f32) * VOCAB ** (-0.5)
        inp['bin'] = jnp.zeros((DIM,), f32)
        inp['ln1_w'] = jnp.ones((DEPTH, DIM), f32)
        inp['ln1_b'] = jnp.zeros((DEPTH, DIM), f32)
        ang = 2 * np.pi * jnp.arange(DIM, dtype=f32) / DIM
        mag = jnp.abs(jax.random.normal(ks[2], (DEPTH, DIM), dtype=f32))
        inp['phz_re'] = mag * jnp.cos(ang)[None]
        inp['phz_im'] = mag * jnp.sin(ang)[None]
        inp['lc_re'] = jax.random.normal(ks[3], (DEPTH, DIM), dtype=f32)
        inp['lc_im'] = jax.random.normal(ks[4], (DEPTH, DIM), dtype=f32)
        inp['sc_lin'] = jnp.ones((DEPTH, DIM), f32)
        inp['ln2_w'] = jnp.ones((DEPTH, DIM), f32)
        inp['ln2_b'] = jnp.zeros((DEPTH, DIM), f32)
        inp['W1'] = jax.random.normal(ks[5], (DEPTH, DFF, DIM), dtype=f32) * DIM ** (-0.5)
        inp['b1'] = jnp.zeros((DEPTH, DFF), f32)
        inp['W2'] = jax.random.normal(ks[6], (DEPTH, DIM, DFF), dtype=f32) * DFF ** (-0.5)
        inp['b2'] = jnp.zeros((DEPTH, DIM), f32)
        inp['lnl_w'] = jnp.ones((DIM,), f32)
        inp['lnl_b'] = jnp.zeros((DIM,), f32)
        inp['Wout'] = jax.random.normal(ks[7], (VOCAB, DIM), dtype=f32) * DIM ** (-0.5)
        inp['bout'] = jnp.zeros((VOCAB,), f32)
        return inp
    _L0_attn_in = _L0_attn_setup()

    def _L0_ffn_setup():
        import jax, jax.numpy as jnp
        import numpy as np
        H, FF = (512, 1792)
        B, S = (4, 256)
        key = jax.random.key(seed)
        ks = jax.random.split(key, 7)
        x = jax.random.normal(ks[0], (B, S, H), dtype=jnp.float32)
        gate_t = jax.random.randint(ks[1], (FF, H), -1, 2, dtype=jnp.int32)
        up_t = jax.random.randint(ks[2], (FF, H), -1, 2, dtype=jnp.int32)
        down_t = jax.random.randint(ks[3], (H, FF), -1, 2, dtype=jnp.int32)
        gate_s = jax.random.uniform(ks[4], (FF,), jnp.float32, 0.01, 0.1)
        up_s = jax.random.uniform(ks[5], (FF,), jnp.float32, 0.01, 0.1)
        down_s = jax.random.uniform(ks[6], (H,), jnp.float32, 0.01, 0.1)
        return {'x': x, 'gate_t': gate_t, 'up_t': up_t, 'down_t': down_t, 'gate_s': gate_s, 'up_s': up_s, 'down_s': down_s}
    _L0_ffn_in = _L0_ffn_setup()

    def _L1_attn_setup():
        import jax, jax.numpy as jnp
        import numpy as np
        BH = 32
        BW = 32
        key = jax.random.key(seed)
        k1, k2, k3, k4 = jax.random.split(key, 4)
        B, S, K, N = (2, 256, 512, 512)
        data = jax.random.normal(k1, (B, S, K), dtype=jnp.float32)
        weight = jax.random.normal(k2, (N, K), dtype=jnp.float32) * 0.02
        bias = jax.random.normal(k3, (N,), dtype=jnp.float32) * 0.02
        Nb, Kb = (N // BH, K // BW)
        block_on = jax.random.uniform(k4, (Nb, Kb)) < 0.3
        mask = jnp.repeat(jnp.repeat(block_on, BH, axis=0), BW, axis=1).astype(jnp.int32)
        return {'data': data, 'mask': mask, 'weight': weight, 'bias': bias}
    _L1_attn_in = _L1_attn_setup()

    def _L1_ffn_setup():
        import jax, jax.numpy as jnp
        import numpy as np
        HIDDEN = 512
        INTER = 1376
        RANK = 128
        B, S = (2, 256)
        key = jax.random.key(seed)
        ks = jax.random.split(key, 7)
        sc = 0.02
        return {'x': jax.random.normal(ks[0], (B, S, HIDDEN), dtype=jnp.float32), 'U1': jax.random.normal(ks[1], (HIDDEN, RANK), dtype=jnp.float32) * sc, 'V1': jax.random.normal(ks[2], (RANK, 2 * INTER), dtype=jnp.float32) * sc, 'U2': jax.random.normal(ks[3], (INTER, RANK), dtype=jnp.float32) * sc, 'V2': jax.random.normal(ks[4], (RANK, HIDDEN), dtype=jnp.float32) * sc, 'b1': jax.random.normal(ks[5], (2 * INTER,), dtype=jnp.float32) * sc, 'b2': jax.random.normal(ks[6], (HIDDEN,), dtype=jnp.float32) * sc}
    _L1_ffn_in = _L1_ffn_setup()
    _d = {'L0_attn_x': _L0_attn_in['x'], 'L0_attn_Win': _L0_attn_in['Win'], 'L0_attn_bin': _L0_attn_in['bin'], 'L0_attn_ln1_w': _L0_attn_in['ln1_w'], 'L0_attn_ln1_b': _L0_attn_in['ln1_b'], 'L0_attn_phz_re': _L0_attn_in['phz_re'], 'L0_attn_phz_im': _L0_attn_in['phz_im'], 'L0_attn_lc_re': _L0_attn_in['lc_re'], 'L0_attn_lc_im': _L0_attn_in['lc_im'], 'L0_attn_sc_lin': _L0_attn_in['sc_lin'], 'L0_attn_ln2_w': _L0_attn_in['ln2_w'], 'L0_attn_ln2_b': _L0_attn_in['ln2_b'], 'L0_attn_W1': _L0_attn_in['W1'], 'L0_attn_b1': _L0_attn_in['b1'], 'L0_attn_W2': _L0_attn_in['W2'], 'L0_attn_b2': _L0_attn_in['b2'], 'L0_attn_lnl_w': _L0_attn_in['lnl_w'], 'L0_attn_lnl_b': _L0_attn_in['lnl_b'], 'L0_attn_Wout': _L0_attn_in['Wout'], 'L0_attn_bout': _L0_attn_in['bout'], 'L0_ffn_gate_t': _L0_ffn_in['gate_t'], 'L0_ffn_up_t': _L0_ffn_in['up_t'], 'L0_ffn_down_t': _L0_ffn_in['down_t'], 'L0_ffn_gate_s': _L0_ffn_in['gate_s'], 'L0_ffn_up_s': _L0_ffn_in['up_s'], 'L0_ffn_down_s': _L0_ffn_in['down_s'], 'L1_attn_mask': _L1_attn_in['mask'], 'L1_attn_weight': _L1_attn_in['weight'], 'L1_attn_bias': _L1_attn_in['bias'], 'L1_ffn_U1': _L1_ffn_in['U1'], 'L1_ffn_V1': _L1_ffn_in['V1'], 'L1_ffn_U2': _L1_ffn_in['U2'], 'L1_ffn_V2': _L1_ffn_in['V2'], 'L1_ffn_b1': _L1_ffn_in['b1'], 'L1_ffn_b2': _L1_ffn_in['b2']}
    _x0 = _d['L0_attn_x']
    _d['L0_attn_x'] = jax.random.normal(jax.random.fold_in(jax.random.key(seed), 1), (4, 256, 512), dtype=_x0.dtype)
    del _x0
    return _d

def reference(L0_attn_x, L0_attn_Win, L0_attn_bin, L0_attn_ln1_w, L0_attn_ln1_b, L0_attn_phz_re, L0_attn_phz_im, L0_attn_lc_re, L0_attn_lc_im, L0_attn_sc_lin, L0_attn_ln2_w, L0_attn_ln2_b, L0_attn_W1, L0_attn_b1, L0_attn_W2, L0_attn_b2, L0_attn_lnl_w, L0_attn_lnl_b, L0_attn_Wout, L0_attn_bout, L0_ffn_gate_t, L0_ffn_up_t, L0_ffn_down_t, L0_ffn_gate_s, L0_ffn_up_s, L0_ffn_down_s, L1_attn_mask, L1_attn_weight, L1_attn_bias, L1_ffn_U1, L1_ffn_V1, L1_ffn_U2, L1_ffn_V2, L1_ffn_b1, L1_ffn_b2):

    def _L0_attn_ref(x, Win, bin, ln1_w, ln1_b, phz_re, phz_im, lc_re, lc_im, sc_lin, ln2_w, ln2_b, W1, b1, W2, b2, lnl_w, lnl_b, Wout, bout):
        import jax, jax.numpy as jnp
        import numpy as np
        DEPTH, DIM, DFF, VOCAB = (4, 64, 256, 512)
        EPS = 1e-05

        def layernorm(x, w, b):
            mu = jnp.mean(x, axis=-1, keepdims=True)
            var = jnp.mean((x - mu) ** 2, axis=-1, keepdims=True)
            return (x - mu) * jax.lax.rsqrt(var + EPS) * w + b

        def sconv(x, phazor_c, last_conv_c):
            B, L, D = x.shape
            r = jnp.abs(phazor_c)
            p = jnp.tanh(r) * jnp.exp(1j * jnp.angle(phazor_c))
            prog = p[None, :] ** jnp.arange(L, dtype=jnp.float32)[:, None]
            filt_fft = jnp.fft.fft(prog, n=2 * L, axis=0)
            x_fft = jnp.fft.fft(x.astype(jnp.complex64), n=2 * L, axis=1)
            conv = jnp.fft.ifft(filt_fft[None] * x_fft, axis=1)[:, :L]
            conv = conv + last_conv_c[None, None, :] * prog[None] * p[None, None, :]
            return conv.real.astype(x.dtype)

        def _forward(x, Win, bin, ln1_w, ln1_b, phz_re, phz_im, lc_re, lc_im, sc_lin, ln2_w, ln2_b, W1, b1, W2, b2, lnl_w, lnl_b, Wout, bout):
            h = jnp.einsum('blv,dv->bld', x, Win) + bin

            def body(h, p):
                l1w, l1b, pr, pi, lr, li, scl, l2w, l2b, w1, b1_, w2, b2_ = p
                y = jax.nn.silu(layernorm(h, l1w, l1b))
                y = sconv(y, pr + 1j * pi, lr + 1j * li)
                h = h + y * scl
                y = layernorm(h, l2w, l2b)
                y = jax.nn.silu(jnp.einsum('bld,fd->blf', y, w1) + b1_)
                y = jnp.einsum('blf,df->bld', y, w2) + b2_
                return (h + y, None)
            xs = (ln1_w, ln1_b, phz_re, phz_im, lc_re, lc_im, sc_lin, ln2_w, ln2_b, W1, b1, W2, b2)
            h, _ = jax.lax.scan(body, h, xs)
            h = layernorm(h, lnl_w, lnl_b)
            return jnp.einsum('bld,vd->blv', h, Wout) + bout
        return _forward(x, Win, bin, ln1_w, ln1_b, phz_re, phz_im, lc_re, lc_im, sc_lin, ln2_w, ln2_b, W1, b1, W2, b2, lnl_w, lnl_b, Wout, bout)

    def _L0_ffn_ref(x, gate_t, up_t, down_t, gate_s, up_s, down_s):
        import jax, jax.numpy as jnp
        import numpy as np
        H, FF = (512, 1792)
        B, S = (4, 256)
        Bb, Ss, Hh = x.shape
        x_flat = x.reshape(Bb * Ss, Hh)
        gate_w = gate_t.astype(jnp.float32) * gate_s[:, None]
        up_w = up_t.astype(jnp.float32) * up_s[:, None]
        down_w = down_t.astype(jnp.float32) * down_s[:, None]
        gate_out = x_flat @ gate_w.T
        up_out = x_flat @ up_w.T
        hidden = jax.nn.silu(gate_out) * up_out
        out_flat = hidden @ down_w.T
        return out_flat.reshape(Bb, Ss, -1)

    def _L1_attn_ref(data, mask, weight, bias):
        import jax, jax.numpy as jnp
        import numpy as np
        BH = 32
        BW = 32
        N, K = weight.shape
        Nb, Kb = (N // BH, K // BW)
        bm = mask.reshape(Nb, BH, Kb, BW).sum(axis=(1, 3)) > 0
        wb = weight.reshape(Nb, BH, Kb, BW) * bm[:, None, :, None].astype(weight.dtype)
        w = wb.reshape(N, K)
        out = jnp.einsum('bsk,nk->bsn', data, w) + bias
        return out

    def _L1_ffn_ref(x, U1, V1, U2, V2, b1, b2):
        import jax, jax.numpy as jnp
        import numpy as np
        HIDDEN = 512
        INTER = 1376
        RANK = 128
        B, S = (2, 256)
        P = jnp.einsum('bsh,hr->bsr', x, U1)
        H = jnp.einsum('bsr,rf->bsf', P, V1) + b1
        gate, up = (H[..., :INTER], H[..., INTER:])
        act = jax.nn.silu(gate) * up
        Z = jnp.einsum('bsi,ir->bsr', act, U2)
        out = jnp.einsum('bsr,rh->bsh', Z, V2) + b2
        return out
    x = L0_attn_x
    xn = _layernorm(x, axis=-1)
    x = x + _L0_attn_ref(xn, L0_attn_Win, L0_attn_bin, L0_attn_ln1_w, L0_attn_ln1_b, L0_attn_phz_re, L0_attn_phz_im, L0_attn_lc_re, L0_attn_lc_im, L0_attn_sc_lin, L0_attn_ln2_w, L0_attn_ln2_b, L0_attn_W1, L0_attn_b1, L0_attn_W2, L0_attn_b2, L0_attn_lnl_w, L0_attn_lnl_b, L0_attn_Wout, L0_attn_bout) + _L0_ffn_ref(xn, L0_ffn_gate_t, L0_ffn_up_t, L0_ffn_down_t, L0_ffn_gate_s, L0_ffn_up_s, L0_ffn_down_s)
    xn = _layernorm(x, axis=-1)
    x = x + _L1_attn_ref(xn, L1_attn_mask, L1_attn_weight, L1_attn_bias) + _L1_ffn_ref(xn, L1_ffn_U1, L1_ffn_V1, L1_ffn_U2, L1_ffn_V2, L1_ffn_b1, L1_ffn_b2)
    return x

_drawn_inputs = setup_inputs


def setup_inputs(seed=0):
    import zlib

    import numpy as np

    out = dict(_drawn_inputs(seed))
    spreads = {'L0_attn_bin': (0.0, 0.1),
     'L0_attn_ln1_w': (1.0, 0.2),
     'L0_attn_ln1_b': (0.0, 0.1),
     'L0_attn_sc_lin': (1.0, 0.2),
     'L0_attn_ln2_w': (1.0, 0.2),
     'L0_attn_ln2_b': (0.0, 0.401),
     'L0_attn_b1': (0.0, 0.482),
     'L0_attn_b2': (0.0, 0.1),
     'L0_attn_lnl_w': (1.0, 0.2),
     'L0_attn_lnl_b': (0.0, 0.1),
     'L0_attn_bout': (0.0, 0.1)}
    factors = {'L1_attn_bias': 200.0,
     'L1_ffn_U1': 8.0,
     'L1_ffn_V1': 8.0,
     'L1_ffn_U2': 8.0,
     'L1_ffn_V2': 8.0,
     'L1_ffn_b1': 8.0,
     'L1_ffn_b2': 200.0,
     'L1_attn_weight': 64.0}
    for name, (base, spread) in spreads.items():
        noise = np.random.default_rng([zlib.crc32(name.encode()), seed]).standard_normal(out[name].shape)
        drawn = base * np.exp(spread * noise) if base else spread * noise
        out[name] = jnp.asarray(drawn.astype(out[name].dtype))
    for name, factor in factors.items():
        out[name] = (out[name] * factor).astype(out[name].dtype)
    return out
```

```python
from contextlib import ExitStack

import concourse.bass as bass
from concourse import mybir

F32 = mybir.dt.float32
F32R = mybir.dt.float32r
F16 = mybir.dt.float16
I32 = mybir.dt.int32
ALU = mybir.AluOpType
ACT = mybir.ActivationFunctionType
AX = mybir.AxisListType

P = 128
NTOK, D = 1024, 512
NBLK = 2
BT = NTOK // NBLK
TPB = BT // P
KT = D // P
SEQ = 256
SPB = BT // SEQ
DEPTH, DIM, DFF = 4, 64, 256
FH = DFF // P
FF = 1792
FT = FF // P
INTER, RANK = 1376, 128
IT = -(-INTER // P)
MB = 32
EPS = 1e-5
SEED = 1597463007.0
NSTAGE = 6
RING = 6
DPIECES = 4

COLS = {}
_n = 0
for _name, _w in (("ident", P), ("blockones", P), ("twoeye", DIM), ("ones", P), ("sign", 1),
                  ("gate_s", FT), ("up_s", FT), ("ln1_w", DEPTH), ("ln1_b", DEPTH),
                  ("re", DEPTH), ("im", DEPTH), ("lc_p", DEPTH), ("lc_q", DEPTH), ("scl", DEPTH),
                  ("ln2_w", DEPTH), ("ln2_b", DEPTH), ("lnl_w", 1), ("lnl_b", 1),
                  ("b1", DEPTH * FH), ("fb_gate", IT), ("fb_up", IT),
                  ("win", KT * DIM), ("w2", DEPTH * FH * DIM)):
    COLS[_name] = (_n, _n + _w)
    _n += _w
NCOL = _n


def chunks_of(total):
    return [(c, min(c + D, total)) for c in range(0, total, D)]


V1_CHUNKS = chunks_of(2 * INTER)
U2_CHUNKS = chunks_of(IT * RANK)


def build_order():
    def ln_big(layer, b):
        return ([("stats", layer, b, t) for t in range(TPB)] + [("rstd", layer, b)]
                + [("norm", layer, b, t) for t in range(TPB)])

    def chain(b):
        jobs = [[("win", b), ("ln", b)]]
        for l in range(DEPTH):
            jobs += [[("t1", b, l)], [("scan", b, l)], [("z", b, l), ("ln", b)],
                     [("t3", b, l)], [("w1", b, l)], [("w2", b, l), ("ln", b)]]
        jobs += [[("tf", b)], [("wo", b, 0), ("wo", b, 1)], [("wo", b, 2), ("wo", b, 3)]]
        return jobs

    slots = []
    for b in range(NBLK):
        for f in range(FT):
            slots += [[("gate", b, f)], [("up", b, f)]]
        for t in range(TPB):
            slots += [[("down", b, t, q)] for q in range(DPIECES)]
    n_slots = len(slots)
    after = [[] for _ in slots]
    up_at = lambda b, f: b * (n_slots // 2) + 2 * f + 1

    for f in range(FT):
        if f + 2 < FT:
            after[up_at(0, f) - 1].append(("cast", "gate", f + 2))
            after[up_at(0, f)].append(("cast", "up", f + 2))
        after[up_at(0, f)].append(("cast", "down", f))
    pieces = ln_big(0, 1)
    for i, p in enumerate(pieces):
        after[1 + i // 2].append(p)
    for t in range(TPB):
        after[6 + t].append(("xt", 1, t))
    after[10].append(("xbias", 1))
    last = {}
    for b, start in ((0, 1), (1, 11)):
        s = float(start)
        step = CHAIN_STEP[b]
        for job in chain(b):
            i = min(int(s), n_slots - 1)
            after[i] += job
            last[b] = i
            s += 1.0 if job[0][0] == "t1" else step
    first_b = n_slots // 2
    for k in range(KT):
        after[first_b + 1 + k].append(("cast", "mask", k))
    after[first_b + 6].append(("maskones",))
    after[first_b + 7].append(("cast", "U1", 0))
    gu_end = first_b + 2 * FT
    for i in range(len(V1_CHUNKS)):
        after[gu_end + 1 + 2 * i].append(("cast", "V1", i))

    assert last[0] + TPB + 1 < n_slots
    order = ln_big(0, 0) + [("xt", 0, t) for t in range(TPB)]
    order += [("cast", k, f) for f in range(2) for k in ("gate", "up")] + [("tables",), ("xbias", 0)]
    for s in range(n_slots):
        order += slots[s] + after[s]
        if s == max(last[0], first_b):
            order += ln_big(1, 0)
        elif last[0] + 1 <= s <= last[0] + TPB:
            order.append(("yt", 0, s - last[0] - 1))
        elif s == last[0] + TPB + 1:
            order.append(("ybias", 0))
    order += [("u1", 0), ("cast", "U2", 0)]
    for i in range(IT):
        order.append(("hidden", 0, i))
        if i < 2:
            order.append(("cast", "U2", 1 + i))
        elif i < 2 + KT:
            order.append(("cast", "w", i - 2))
        elif i == 2 + KT:
            order.append(("cast", "V2", 0))
        if i == 0:
            order += ln_big(1, 1)
        elif i <= TPB:
            order += [("yt", 1, i - 1)]
        elif i == TPB + 1:
            order += [("ybias", 1)]
    for b in range(NBLK):
        if b:
            order += [("hidden", b, i) for i in range(IT)]
        else:
            order.append(("attn", 0, 0))
        order += [("hidden_end", b), ("attn", b, 1), ("zcopy", b)]
        if b == 0:
            order.append(("u1", 1))
        order += [("out", b, 0), ("out", b, 1), ("attn", b, 2), ("out", b, 2), ("attn", b, 3), ("out", b, 3)]
        if b == 0:
            order.append(("attn", 1, 0))
    return order


CHAIN_STEP = {0: 3.1, 1: 2.8}


def place_psum(order):
    where, turns, n = {}, [0] * (RING + 2), 0
    open_bank = None

    def take(key, bank=None):
        nonlocal n
        if bank is None:
            n += n % RING == open_bank
            bank = n % RING
            n += 1
        turns[bank] += 1
        where[key] = (bank, turns[bank])

    for step in order:
        kind = step[0]
        if kind in ("xt", "yt", "t1", "t3", "tf", "wo", "maskones", "gate", "up", "u1"):
            take(step)
        elif kind == "down":
            key = ("down", *step[1:3])
            if step[3] == 0:
                take(key)
            open_bank = where[key][0] if step[3] < DPIECES - 1 else None
        elif kind == "w1":
            for half in range(FH):
                take((*step, half))
        elif kind == "hidden":
            take(("hgate", *step[1:]))
            take(("hup", *step[1:]))
        elif kind == "attn":
            take(step, RING + 1 if step[2] == 0 else None)
        elif kind == "hidden_end":
            take(("zsum", step[1]), RING)
    return where


def two_layers(nc: bass.Bass, x, gate, up, down, mask, weight, v1, u2, u1, v2, params, wide64,
               rows, rows64, out):
    order = build_order()
    psum_at = place_psum(order)
    casts = [s[1:] for s in order if s[0] == "cast"]
    ternary = [c for c in casts if c[0] in ("gate", "up", "down")]
    general = [c for c in casts if c[0] in ("U1", "V1", "U2", "w", "V2")]
    source = {"gate": gate, "up": up, "down": down, "mask": mask, "w": weight}

    with ExitStack() as ctx:
        def sb(name, shape, dt=F32, at=ctx):
            return at.enter_context(nc.sbuf_tensor(name, shape, dt))

        def sem(name):
            return ctx.enter_context(nc.semaphore(name))

        def overlay(first, second):
            size = lambda group: sum(w * (2 if dt == F16 else 4) for _, w, dt in group)
            small, large = sorted((first, second), key=size)
            with ExitStack() as s:
                tiles = {n: s.enter_context(nc.sbuf_tensor(n, [P, w], dt)) for n, w, dt in small}
            tiles |= {n: ctx.enter_context(nc.sbuf_tensor(n, [P, w], dt)) for n, w, dt in large}
            return tiles

        X = sb("X", [P, NTOK // P, D])
        XN = sb("XN", [P, TPB, D])
        stage = sb("stage", [P, NSTAGE, D], I32)
        prm = sb("prm", [P, NCOL])
        w64 = sb("w64", [DIM, DEPTH * DFF + D])
        w1t = w64[:, 0:DEPTH * DFF].rearrange("p (l f) -> p l f", l=DEPTH)
        woutt = w64[:, DEPTH * DFF:]
        bc = sb("bc", [P, 4, D])
        row64 = sb("row64", [1, DEPTH + 1, DIM])
        r0 = overlay([("XT", KT * BT, F32), ("xh0", KT * BT, F16), ("xl0", KT * BT, F16)],
                     [("yh0", KT * BT, F32R), ("yl0", KT * BT, F32R)])
        xb1 = [sb(n, [P, KT, BT], F16) for n in ("xh1", "xl1")]
        r1 = overlay([("gatew", FT * D, F16), ("upw", FT * D, F16)],
                     [("V1h", 2 * INTER, F32R), ("V1l", 2 * INTER, F32R)])
        r2 = overlay([("hidh", FT * BT, F16), ("hidl", FT * BT, F16)],
                     [("yh1", KT * BT, F32R), ("yl1", KT * BT, F32R),
                      ("acth", 2 * BT, F32R), ("actl", 2 * BT, F32R)])
        r3 = overlay([("downw", FT * D, F16)],
                     [("U2h", IT * RANK, F32R), ("U2l", IT * RANK, F32R)])
        mini = []
        for b in range(NBLK):
            mini += [(f"lno{b}", TPB * P, F32), (f"ymini{b}", BT, F32), (f"uscan{b}", BT, F32),
                     (f"yff{b}", FH * BT, F32)]
        r4 = overlay(mini + [("rot", DEPTH * 2 * (SEQ + 1), F32)],
                     [("Wh", KT * D, F32R), ("Wl", KT * D, F32R), ("V2h", D, F32R), ("V2l", D, F32R),
                      ("ph", BT, F32R), ("pl", BT, F32R), ("zh", BT, F32R), ("zl", BT, F32R)])
        U1h, U1l = sb("U1h", [P, KT * RANK], F32R), sb("U1l", [P, KT * RANK], F32R)
        silu = sb("silu", [P, 2, BT])
        hid = sb("hid", [P, 2, BT])
        tmp = sb("tmp", [P, D])
        st = sb("st", [P, TPB, 6])
        mv = sb("mv", [P, TPB, 2])
        mvs = [sb(f"mvs{b}", [P, TPB, 2]) for b in range(NBLK)]
        nv, ny, na = (sb(n, [P, TPB]) for n in ("nv", "ny", "na"))
        rot_t = sb("rot_t", [P, DEPTH, 2, SEQ // 2])
        pz = sb("pz", [P, 8, DEPTH])
        scan0 = sb("scan0", [P, DEPTH])
        rad = sb("rad", [P, DEPTH])
        msum = sb("msum", [P, KT * D // MB])
        m01 = sb("m01", [P, KT * D // MB])

        tile = lambda group, name, a: group[name][:].rearrange("p (a n) -> p a n", a=a)
        XT = tile(r0, "XT", KT)
        xh = [tile(r0, "xh0", KT), xb1[0][:]]
        xl = [tile(r0, "xl0", KT), xb1[1][:]]
        yh = [tile(r0, "yh0", KT), tile(r2, "yh1", KT)]
        yl = [tile(r0, "yl0", KT), tile(r2, "yl1", KT)]
        codes = {"gate": tile(r1, "gatew", FT), "up": tile(r1, "upw", FT), "down": tile(r3, "downw", FT)}
        hidh, hidl = tile(r2, "hidh", FT), tile(r2, "hidl", FT)
        acth, actl = tile(r2, "acth", 2), tile(r2, "actl", 2)
        lno = [tile(r4, f"lno{b}", TPB) for b in range(NBLK)]
        ymini = [r4[f"ymini{b}"][:] for b in range(NBLK)]
        uscan = [r4[f"uscan{b}"][:] for b in range(NBLK)]
        yff = [tile(r4, f"yff{b}", FH) for b in range(NBLK)]
        rot = r4["rot"][:].rearrange("p (l c t) -> p l c t", l=DEPTH, c=2)
        Wh, Wl = tile(r4, "Wh", KT), tile(r4, "Wl", KT)
        split = {"U1": (U1h[:], U1l[:]), "V1": (r1["V1h"][:], r1["V1l"][:]),
                 "U2": (r3["U2h"][:], r3["U2l"][:]), "V2": (r4["V2h"][:], r4["V2l"][:]),
                 "w": (r4["Wh"][:], r4["Wl"][:])}
        ph, pl, zh, zl = (r4[n][:] for n in ("ph", "pl", "zh", "zl"))

        def col(name, i=0, n=1):
            return prm[:, COLS[name][0] + i:COLS[name][0] + i + n]

        ident, twoeye = col("ident", 0, P), col("twoeye", 0, DIM)
        winT = col("win", 0, KT * DIM).rearrange("p (k d) -> p k d", k=KT)
        w2T = col("w2", 0, DEPTH * FH * DIM).rearrange("p (l h d) -> p l h d", l=DEPTH, h=FH)
        DOWN_S, BOUT, BIAS1, BIAS2 = range(4)

        banks = [ctx.enter_context(nc.psum_tensor(f"bank{i}", [P, D], F32)) for i in range(RING + 2)]
        h = [banks[RING + b][:, 0:TPB * DIM].rearrange("p (t d) -> p t d", t=TPB) for b in range(NBLK)]

        x_in = [sem(f"x_in{t}") for t in range(NTOK // P)]
        prm_in, w64_in, bc_in, row64_in = sem("prm_in"), sem("w64_in"), sem("bc_in"), sem("row64_in")
        stage_in = [sem(f"stage_in{i}") for i in range(NSTAGE)]
        full = [sem(f"psum_full{i}") for i in range(RING + 2)]
        dve_chain, pool_chain = sem("dve_chain"), sem("pool_chain")
        xn_ready = sem("xn_ready")
        xt_hi, xt_lo = sem("xt_hi"), sem("xt_lo")
        yt_hi, yt_lo = sem("yt_hi"), sem("yt_lo")
        x_biased, y_biased = sem("x_biased"), sem("y_biased")
        codes_ready = sem("codes_ready")
        part_hi, part_lo = sem("part_hi"), sem("part_lo")
        masked = sem("masked")
        mask_on = sem("mask_on")
        silu_ready = sem("silu_ready")
        hid_ready = sem("hid_ready")
        hid_hi, hid_lo = sem("hid_hi"), sem("hid_lo")
        h_full = [sem(f"h_full{b}") for b in range(NBLK)]
        ln_ready = [sem(f"ln_ready{b}") for b in range(NBLK)]
        y_ready = [sem(f"y_ready{b}") for b in range(NBLK)]
        z_ready = [sem(f"z_ready{b}") for b in range(NBLK)]
        ff_ready = [sem(f"ff_ready{b}") for b in range(NBLK)]
        size_ready, rad_ready = sem("size_ready"), sem("rad_ready")
        tables_ready = sem("tables_ready")
        p_hi, p_lo, z_hi, z_lo = sem("p_hi"), sem("p_lo"), sem("z_hi"), sem("z_lo")
        out_ready, out_done = sem("out_ready"), sem("out_done")
        down_read = sem("down_read")
        wo_added = [sem(f"wo_added{b}") for b in range(NBLK)]
        act_used = sem("act_used")
        rot_seed = sem("rot_seed")

        def wait_full(eng, key):
            bank, turn = psum_at[key]
            eng.wait_ge(full[bank], turn)

        def released(key):
            kind, b, *rest = key if len(key) > 1 else (*key, 0)
            at = b * TPB + (rest[0] if rest else 0) + 1
            return {
                "xt": lambda: (xt_hi, at),
                "yt": lambda: (yt_lo, at),
                "t1": lambda: (y_ready[b], 2 * rest[0] + 1),
                "t3": lambda: (y_ready[b], 2 * rest[0] + 2),
                "tf": lambda: (y_ready[b], 2 * DEPTH + 1),
                "w1": lambda: (ff_ready[b], FH * rest[0] + rest[1] + 1),
                "wo": lambda: (wo_added[b], rest[0] + 1),
                "gate": lambda: (silu_ready, unit(b, rest[0]) + 1),
                "up": lambda: (hid_ready, unit(b, rest[0]) + 1),
                "down": lambda: (down_read, at),
                "maskones": lambda: (mask_on, 1),
                "u1": lambda: (p_lo, b + 1),
                "hgate": lambda: (silu_ready, unit1(b, rest[0]) + 1),
                "hup": lambda: (hid_ready, unit1(b, rest[0]) + 1),
                "zsum": lambda: (z_lo, b + 1),
                "attn": lambda: (out_ready, at),
            }[kind]()

        tenant = {v: k for k, v in psum_at.items()}

        def wait_bank(pe, key):
            bank, turn = psum_at[key]
            if turn > 1:
                pe.wait_ge(*released(tenant[bank, turn - 1]))

        def bank_of(key):
            return banks[psum_at[key][0]]

        def full_of(key):
            return full[psum_at[key][0]]

        def landed(eng, cast):
            n = casts.index(cast)
            eng.wait_ge(stage_in[n % NSTAGE], 16 * (n // NSTAGE + 1))

        def slot(cast):
            return casts.index(cast) % NSTAGE

        def chunk_range(kind, i):
            c0, c1 = {"V1": V1_CHUNKS, "U2": U2_CHUNKS}[kind][i] if kind in ("V1", "U2") else \
                (i * D, (i + 1) * D)
            return c0, c1

        def unit(b, f):
            return b * FT + f

        def unit1(b, i):
            return NBLK * FT + b * IT + i

        rows_of = lambda i: min(P, INTER - i * P)
        ln_count = 2 * DEPTH + 1

        block = ctx.enter_context(nc.Block())

        @block.sync
        def _(sp):
            for t in range(TPB):
                sp.dma_start(X[:, t, :], x[t]).then_inc(x_in[t], 16)
                if t == 1:
                    sp.dma_start(prm[:], params).then_inc(prm_in, 16)

            def load(n):
                kind, i = casts[n]
                if n >= NSTAGE:
                    before = casts[n - NSTAGE]
                    if before in ternary:
                        sp.wait_ge(codes_ready, ternary.index(before) + 1)
                    elif before in general:
                        sp.wait_ge(part_lo, general.index(before) + 1)
                    else:
                        sp.wait_ge(masked, before[1] + 1)
                if kind in ("V1", "U2"):
                    c0, c1 = chunk_range(kind, i)
                    src = (v1 if kind == "V1" else u2)[:, c0:c1]
                elif kind in ("U1", "V2"):
                    src, c0, c1 = (u1 if kind == "U1" else v2), 0, D
                else:
                    src, c0, c1 = source[kind][i], 0, D
                dst = stage[:, n % NSTAGE, 0:c1 - c0]
                if kind not in ("gate", "up", "down", "mask"):
                    dst = dst.bitcast(F32)
                sp.dma_start(dst, src).then_inc(stage_in[n % NSTAGE], 16)

            for n in range(4):
                load(n)
            sp.dma_start(w64[:], wide64).then_inc(w64_in, 16)
            sp.dma_start(row64[:], rows64).then_inc(row64_in, 16)
            sp.dma_start(bc[:], rows.partition_broadcast(P)).then_inc(bc_in, 16)
            for t in range(TPB, 2 * TPB):
                sp.dma_start(X[:, t, :], x[t]).then_inc(x_in[t], 16)
            for n in range(4, len(casts)):
                load(n)
            for t in range(NTOK // P):
                sp.wait_ge(out_ready, t + 1)
                sp.dma_start(out[t], X[:, t, :]).then_inc(out_done, 16)
            sp.wait_ge(out_done, 16 * (NTOK // P))

        @block.tensor
        def _(pe):
            def transpose_tile(key, ready, count):
                wait_bank(pe, key)
                pe.wait_ge(ready, count)
                for k in range(KT):
                    mm = pe.transpose(bank_of(key)[:, k * P:(k + 1) * P],
                                      XN[:, key[2], k * P:(k + 1) * P], ident)
                mm.then_inc(full_of(key), 1)

            def three_passes(dst, lhs, rhs, first, last):
                pe.matmul(dst, lhs[0], rhs[0], start=first, stop=False)
                pe.matmul(dst, lhs[0], rhs[1], start=False, stop=False)
                return pe.matmul(dst, lhs[1], rhs[0], start=False, stop=last)

            def low_rank_down(b, i):
                n = unit1(b, i)
                pe.wait_ge(hid_lo, n + 1)
                if i == 0:
                    if b == 0:
                        pe.wait_ge(part_lo, general.index(("U2", 0)) + 1)
                        pe.wait_ge(ln_ready[0], ln_count)
                    else:
                        pe.wait_ge(z_lo, 1)
                if b == 0 and i * RANK // D > 0:
                    pe.wait_ge(part_lo, general.index(("U2", i * RANK // D)) + 1)
                K, c = rows_of(i), slice(i * RANK, (i + 1) * RANK)
                mm = three_passes(banks[RING][:], [w[0:K, c] for w in split["U2"]],
                                  [a[0:K, n % 2, :] for a in (acth, actl)], i == 0, i == IT - 1)
                return mm.then_inc(full[RING] if i == IT - 1 else act_used, 1)

            pe.wait_ge(prm_in, 16)
            for step in order:
                kind = step[0]
                if kind in ("xt", "yt"):
                    layer = 0 if kind == "xt" else 1
                    transpose_tile(step, xn_ready, (layer * NBLK + step[1]) * TPB + step[2] + 1)
                elif kind == "win":
                    b = step[1]
                    pe.wait_ge(xt_hi, TPB * (b + 1))
                    pe.wait_ge(row64_in, 16)
                    for t in range(TPB):
                        for k in range(KT):
                            pe.matmul(h[b][:, t, :], XT[:, k, t * P:(t + 1) * P], winT[:, k, :],
                                      start=(t == 0 and k == 0), stop=False, skip_group_check=True)
                        mm = pe.matmul(h[b][:, t, :], col("ones", 0, P)[0:1, :], row64[0:1, DEPTH, :],
                                       start=False, stop=False, skip_group_check=True)
                    mm.then_inc(h_full[b], 1)
                elif kind in ("t1", "t3", "tf"):
                    b = step[1]
                    count = DEPTH * 2 + 1 if kind == "tf" else 2 * step[2] + (1 if kind == "t1" else 2)
                    wait_bank(pe, step)
                    pe.wait_ge(ln_ready[b], count)
                    w = P if kind == "t1" else DIM
                    for t in range(TPB):
                        mm = pe.transpose(bank_of(step)[0:w, t * P:(t + 1) * P], lno[b][:, t, 0:w], ident)
                    mm.then_inc(full_of(step), 1)
                elif kind == "z":
                    _, b, l = step
                    pe.wait_ge(z_ready[b], l + 1)
                    for t in range(TPB):
                        mm = pe.matmul(h[b][:, t, :], ymini[b][:, t * P:(t + 1) * P], twoeye,
                                       start=False, stop=False, skip_group_check=True)
                    mm.then_inc(h_full[b], 1)
                elif kind == "w1":
                    _, b, l = step
                    pe.wait_ge(y_ready[b], 2 * l + 2)
                    pe.wait_ge(w64_in, 16)
                    for half in range(FH):
                        key = (*step, half)
                        wait_bank(pe, key)
                        pe.matmul(bank_of(key)[:], w1t[:, l, half * P:(half + 1) * P], ymini[b][0:DIM, :],
                                  start=True, stop=True).then_inc(full_of(key), 1)
                elif kind == "w2":
                    _, b, l = step
                    pe.wait_ge(ff_ready[b], FH * (l + 1))
                    for t in range(TPB):
                        pe.matmul(h[b][:, t, :], col("ones", 0, P)[0:1, :], row64[0:1, l, :],
                                  start=False, stop=False, skip_group_check=True)
                        for half in range(FH):
                            mm = pe.matmul(h[b][:, t, :], yff[b][:, half, t * P:(t + 1) * P],
                                           w2T[:, l, half, :], start=False, stop=False,
                                           skip_group_check=True)
                    mm.then_inc(h_full[b], 1)
                elif kind == "wo":
                    _, b, t = step
                    wait_bank(pe, step)
                    pe.wait_ge(y_ready[b], 2 * DEPTH + 1)
                    pe.matmul(bank_of(step)[:], ymini[b][0:DIM, t * P:(t + 1) * P], woutt,
                              start=True, stop=True).then_inc(full_of(step), 1)
                elif kind in ("gate", "up"):
                    _, b, f = step
                    wait_bank(pe, step)
                    pe.wait_ge(codes_ready, ternary.index((kind, f)) + 1)
                    pe.wait_ge(xt_lo, TPB * (b + 1))
                    for k in range(KT):
                        w = codes[kind][:, f, k * P:(k + 1) * P]
                        pe.matmul(bank_of(step)[:], w, xh[b][:, k, :], start=(k == 0), stop=False)
                        mm = pe.matmul(bank_of(step)[:], w, xl[b][:, k, :], start=False, stop=(k == KT - 1))
                    mm.then_inc(full_of(step), 1)
                elif kind == "down":
                    _, b, t, q = step
                    key = ("down", b, t)
                    if q == 0:
                        wait_bank(pe, key)
                        if t == 0:
                            pe.wait_ge(codes_ready, len(ternary))
                    edges = [FT * i // DPIECES for i in range(DPIECES + 1)]
                    for f in range(edges[q], edges[q + 1]):
                        if t == 0:
                            pe.wait_ge(hid_lo, unit(b, f) + 1)
                        for part in (hidh, hidl):
                            mm = pe.matmul(bank_of(key)[:], part[:, f, t * P:(t + 1) * P],
                                           codes["down"][:, f, :], start=(f == 0 and part is hidh),
                                           stop=(f == FT - 1 and part is hidl))
                    if q == DPIECES - 1:
                        mm.then_inc(full_of(key), 1)
                elif kind == "maskones":
                    wait_bank(pe, step)
                    pe.wait_ge(masked, KT)
                    pe.matmul(bank_of(step)[:, 0:KT * D // MB], col("blockones", 0, P), msum[:],
                              start=True, stop=True).then_inc(full_of(step), 1)
                elif kind == "u1":
                    b = step[1]
                    wait_bank(pe, step)
                    pe.wait_ge(yt_lo, TPB * (b + 1))
                    pe.wait_ge(part_lo, general.index(("U1", 0)) + 1)
                    for k in range(KT):
                        c = slice(k * RANK, (k + 1) * RANK)
                        mm = three_passes(bank_of(step)[:], [w[:, c] for w in split["U1"]],
                                          [yh[b][:, k, :], yl[b][:, k, :]], k == 0, k == KT - 1)
                    mm.then_inc(full_of(step), 1)
                elif kind == "hidden":
                    _, b, i = step
                    if i == 0:
                        pe.wait_ge(p_lo, b + 1)
                    if b == 0:
                        pe.wait_ge(part_lo, general.index(("V1", (INTER + i * P + rows_of(i) - 1) // D)) + 1)
                    for key, off in ((("hgate", b, i), 0), (("hup", b, i), INTER)):
                        wait_bank(pe, key)
                        c = slice(off + i * P, off + i * P + rows_of(i))
                        three_passes(bank_of(key)[0:rows_of(i), :], [w[:, c] for w in split["V1"]],
                                     [ph, pl], True, True).then_inc(full_of(key), 1)
                    if i >= 2:
                        low_rank_down(b, i - 2)
                elif kind == "hidden_end":
                    b = step[1]
                    low_rank_down(b, IT - 2)
                    low_rank_down(b, IT - 1)
                elif kind == "attn":
                    _, b, t = step
                    wait_bank(pe, step)
                    if b == 0:
                        pe.wait_ge(part_lo, len(general))
                    if (b, t) == (0, 0):
                        pe.wait_ge(ln_ready[1], ln_count)
                    c = slice(t * P, (t + 1) * P)
                    for k in range(KT):
                        three_passes(bank_of(step)[:], [yh[b][:, k, c], yl[b][:, k, c]],
                                     [Wh[:, k, :], Wl[:, k, :]], k == 0, False)
                elif kind == "out":
                    _, b, t = step
                    pe.wait_ge(z_lo, b + 1)
                    c = slice(t * P, (t + 1) * P)
                    key = ("attn", b, t)
                    three_passes(bank_of(key)[:], [zh[:, c], zl[:, c]], split["V2"],
                                 False, True).then_inc(full_of(key), 1)

        @block.scalar
        def _(act):
            def hidden_hi(n):
                act.wait_ge(hid_ready, n + 1)
                if n < NBLK * FT:
                    if n == FT:
                        wait_full(act, ("down", 0, TPB - 1))
                    act.activation(hidh[:, n % FT, :], hid[:, n % 2, :], ACT.Copy).then_inc(hid_hi, 1)
                else:
                    b, i = divmod(n - NBLK * FT, IT)
                    K = rows_of(i)
                    if i >= 2:
                        act.wait_ge(act_used, b * (IT - 1) + i - 1)
                    act.activation(acth[0:K, n % 2, :], hid[0:K, n % 2, :], ACT.Copy).then_inc(hid_hi, 1)

            act.wait_ge(prm_in, 16)
            for step in order:
                kind = step[0]
                if kind == "xt":
                    _, b, t = step
                    if b == 1 and t == 0:
                        act.wait_ge(h_full[0], 1)
                        act.wait_ge(xt_lo, TPB)
                    wait_full(act, step)
                    src = bank_of(step)[:].rearrange("p (k n) -> p k n", k=KT)
                    c = slice(t * P, (t + 1) * P)
                    act.activation(xh[b][:, :, c], src, ACT.Copy)
                    act.activation(XT[:, :, c], src, ACT.Copy).then_inc(xt_hi, 1)
                elif kind == "tables":
                    act.wait_ge(size_ready, 1)
                    act.activation(rad[:], pz[:, 1, :], ACT.Tanh).then_inc(rad_ready, 1)
                elif kind == "yt":
                    _, b, t = step
                    wait_full(act, step)
                    src = bank_of(step)[:].rearrange("p (k n) -> p k n", k=KT)
                    act.activation(yh[b][:, :, t * P:(t + 1) * P], src, ACT.Copy).then_inc(yt_hi, 1)
                elif kind == "t1":
                    _, b, l = step
                    wait_full(act, step)
                    act.activation(ymini[b], bank_of(step)[:], ACT.Silu, bias=col("ln1_b", l),
                                   scale=col("ln1_w", l)).then_inc(y_ready[b], 1)
                elif kind in ("t3", "tf"):
                    b = step[1]
                    w, c = (col("ln2_w", step[2]), col("ln2_b", step[2])) if kind == "t3" else \
                        (col("lnl_w"), col("lnl_b"))
                    wait_full(act, step)
                    act.activation(ymini[b][0:DIM, :], bank_of(step)[0:DIM, :], ACT.Identity,
                                   bias=c[0:DIM, :], scale=w[0:DIM, :]).then_inc(y_ready[b], 1)
                elif kind == "w1":
                    _, b, l = step
                    for half in range(FH):
                        key = (*step, half)
                        wait_full(act, key)
                        act.activation(yff[b][:, half, :], bank_of(key)[:], ACT.Silu,
                                       bias=col("b1", l * FH + half)).then_inc(ff_ready[b], 1)
                elif kind == "gate":
                    _, b, f = step
                    n = unit(b, f)
                    if n >= 2:
                        act.wait_ge(hid_ready, n - 1)
                    wait_full(act, step)
                    act.activation(silu[:, n % 2, :], bank_of(step)[:], ACT.Silu,
                                   scale=col("gate_s", f)).then_inc(silu_ready, 1)
                    if f >= 1:
                        hidden_hi(n - 1)
                elif kind == "down" and step[2:] == (0, 0):
                    hidden_hi(unit(step[1], FT - 1))
                elif kind == "u1":
                    wait_full(act, step)
                    act.activation(ph, bank_of(step)[:], ACT.Copy).then_inc(p_hi, 1)
                elif kind == "hidden":
                    _, b, i = step
                    n = unit1(b, i)
                    K = rows_of(i)
                    act.wait_ge(hid_ready, n - 1)
                    wait_full(act, ("hgate", b, i))
                    act.activation(silu[0:K, n % 2, :], bank_of(("hgate", b, i))[0:K, :], ACT.Silu,
                                   bias=col("fb_gate", i)[0:K, :]).then_inc(silu_ready, 1)
                    if i >= 1:
                        hidden_hi(n - 1)
                elif kind == "hidden_end":
                    hidden_hi(unit1(step[1], IT - 1))
                elif kind == "zcopy":
                    wait_full(act, ("zsum", step[1]))
                    act.activation(zh, banks[RING][:], ACT.Copy).then_inc(z_hi, 1)

        @block.vector
        def _(dve):
            counts = {}

            def emit(ins, signal=dve_chain):
                counts[id(signal)] = counts.get(id(signal), 0) + 1
                ins.then_inc(signal, 1)
                dve.wait_ge(signal, counts[id(signal)])

            def inverse_root(y, v, n):
                emit(dve.tensor_scalar(y.bitcast(I32), v.bitcast(I32), -0.5, SEED, ALU.mult, ALU.add))
                for _ in range(3):
                    emit(dve.scalar_tensor_tensor(out=na[:, :n], in0=y, scalar=-0.5, in1=y,
                                                  op0=ALU.mult, op1=ALU.mult))
                    emit(dve.tensor_tensor(na[:, :n], na[:, :n], v, ALU.mult))
                    emit(dve.scalar_tensor_tensor(out=y, in0=na[:, :n], scalar=1.5, in1=y,
                                                  op0=ALU.add, op1=ALU.mult))

            def deviations(mv):
                emit(dve.tensor_scalar(nv[:], mv[:, :, 1], EPS, None, ALU.add))
                inverse_root(ny[:], nv[:], TPB)

            mini_norms = [0] * NBLK
            for step in order:
                kind = step[0]
                if kind == "stats":
                    _, layer, b, t = step
                    n = b * TPB + t
                    if layer == 0:
                        dve.wait_ge(x_in[n], 16)
                    emit(dve.bn_stats(st[:, t, :], X[:, n, :]))
                    emit(dve.bn_aggr(mv[:, t, :], st[:, t, :]))
                elif kind == "rstd":
                    deviations(mv)
                elif kind == "norm":
                    _, layer, b, t = step
                    n = b * TPB + t
                    before = layer * NBLK + b - 1
                    if before >= 0:
                        wait_full(dve, ("yt" if before >= NBLK else "xt", before % NBLK, t))
                    emit(dve.tensor_scalar(XN[:, t, :], X[:, n, :], mv[:, t, 0:1], ny[:, t:t + 1],
                                           ALU.subtract, ALU.mult), xn_ready)
                elif kind == "xt":
                    _, b, t = step
                    dve.wait_ge(xt_hi, b * TPB + t + 1)
                    c = slice(t * P, (t + 1) * P)
                    emit(dve.tensor_tensor(xl[b][:, :, c], XT[:, :, c], xh[b][:, :, c], ALU.subtract), xt_lo)
                elif kind == "yt":
                    _, b, t = step
                    dve.wait_ge(yt_hi, b * TPB + t + 1)
                    c = slice(t * P, (t + 1) * P)
                    src = bank_of(step)[:].rearrange("p (k n) -> p k n", k=KT)
                    emit(dve.tensor_tensor(yl[b][:, :, c], src, yh[b][:, :, c].bitcast(F32),
                                           ALU.subtract), yt_lo)
                elif kind == "tables":
                    re, im = col("re", 0, DEPTH), col("im", 0, DEPTH)
                    s2, size, inv, zero, re1, q, c0 = (pz[:, i, :] for i in range(7))
                    dve.wait_ge(prm_in, 16)
                    emit(dve.tensor_tensor(s2, re, re, ALU.mult))
                    emit(dve.tensor_tensor(q, im, im, ALU.mult))
                    emit(dve.tensor_tensor(s2, s2, q, ALU.add))
                    emit(dve.tensor_scalar(zero, s2, 0.0, None, ALU.is_equal))
                    emit(dve.tensor_tensor(nv[:, 0:DEPTH], s2, zero, ALU.add))
                    emit(dve.tensor_tensor(re1, re, zero, ALU.add))
                    inverse_root(inv, nv[:, 0:DEPTH], DEPTH)
                    emit(dve.tensor_tensor(size, s2, inv, ALU.mult), size_ready)
                    emit(dve.tensor_tensor(rot[:, :, 0, 1], re1, inv, ALU.mult))
                    emit(dve.scalar_tensor_tensor(out=rot[:, :, 1, 1], in0=im, scalar=-1.0, in1=inv,
                                                  op0=ALU.mult, op1=ALU.mult))
                    emit(dve.memset(rot[:, :, 0, 0:1], 1.0))
                    emit(dve.memset(rot[:, :, 1, 0:1], 0.0))
                    emit(dve.tensor_tensor(c0, rot[:, :, 0, 1], col("lc_p", 0, DEPTH), ALU.mult))
                    emit(dve.scalar_tensor_tensor(out=q, in0=rot[:, :, 1, 1], scalar=col("sign"),
                                                  in1=col("lc_q", 0, DEPTH), op0=ALU.mult, op1=ALU.mult))
                    emit(dve.tensor_tensor(scan0[:], c0, q, ALU.add), rot_seed)
                elif kind == "ln":
                    b = step[1]
                    k = mini_norms[b]
                    mini_norms[b] += 1
                    dve.wait_ge(h_full[b], k + 1)
                    for t in range(TPB):
                        emit(dve.bn_stats(st[:, t, :], h[b][:, t, :]))
                    for t in range(TPB):
                        emit(dve.bn_aggr(mvs[b][:, t, :], st[:, t, :]))
                    deviations(mvs[b])
                    twice = k % 2 == 0 and k < 2 * DEPTH
                    for t in range(TPB):
                        src, dst = h[b][:, t, :], lno[b][:, t, 0:DIM]
                        if twice:
                            src = src.unsqueeze(1).to_broadcast([P, 2, DIM])
                            dst = lno[b][:, t, :].rearrange("p (c d) -> p c d", c=2)
                        emit(dve.tensor_scalar(dst, src, mvs[b][:, t, 0:1], ny[:, t:t + 1],
                                               ALU.subtract, ALU.mult),
                             ln_ready[b] if t == TPB - 1 else dve_chain)
                elif kind == "scan":
                    _, b, l = step
                    y = ymini[b].rearrange("p (s t) -> p s t", s=SPB)
                    u = uscan[b].rearrange("p (s t) -> p s t", s=SPB)
                    turn = rot[:, l, 0, 0:SEQ].unsqueeze(1).to_broadcast([P, SPB, SEQ])
                    if l == 0:
                        dve.wait_ge(tables_ready, 1)
                        dve.wait_ge(rad_ready, 1)
                    dve.wait_ge(y_ready[b], 2 * l + 1)
                    emit(dve.tensor_tensor(y, y, turn, ALU.mult))
                    for s in range(SPB):
                        emit(dve.tensor_tensor_scan(u[:, s, :], rad[:, l:l + 1].to_broadcast([P, SEQ]),
                                                    y[:, s, :], scan0[:, l:l + 1], ALU.mult, ALU.add))
                    emit(dve.scalar_tensor_tensor(out=y, in0=u, scalar=col("scl", l), in1=turn,
                                                  op0=ALU.mult, op1=ALU.mult), z_ready[b])
                elif kind == "cast":
                    _, what, i = step
                    landed(dve, step[1:])
                    c0, c1 = chunk_range(what, i)
                    src = stage[:, slot(step[1:]), 0:c1 - c0]
                    if what in codes:
                        emit(dve.tensor_copy(codes[what][:, i, :], src), codes_ready)
                    elif what == "mask":
                        nb = D // MB
                        emit(dve.tensor_reduce(msum[:, i * nb:(i + 1) * nb],
                                               src.rearrange("p (a n) -> p a n", n=MB), AX.X, ALU.add),
                             masked)
                    else:
                        src = src.bitcast(F32)
                        if what == "V1" and i == 0:
                            wait_full(dve, ("up", 1, FT - 1))
                        if what == "U2" and i == 0:
                            wait_full(dve, ("down", 1, TPB - 1))
                        if what == "w":
                            if i == 0:
                                wait_full(dve, ("wo", 1, TPB - 1))
                            nb = D // MB
                            on = m01[:, i * nb:(i + 1) * nb].unsqueeze(2).to_broadcast([P, nb, MB])
                            blocks = src.rearrange("p (a n) -> p a n", n=MB)
                            emit(dve.tensor_tensor(blocks, blocks, on, ALU.mult))
                        hi = split[what][0]
                        emit(dve.tensor_copy(hi[:, c0:c1], src), part_hi)
                elif kind == "maskones":
                    wait_full(dve, step)
                    emit(dve.tensor_scalar(m01[:], bank_of(step)[:, 0:KT * D // MB], 0.0, None,
                                           ALU.is_gt), mask_on)
                elif kind == "up":
                    _, b, f = step
                    n = unit(b, f)
                    if n >= 2:
                        dve.wait_ge(hid_lo, n - 1)
                    dve.wait_ge(silu_ready, n + 1)
                    wait_full(dve, step)
                    emit(dve.scalar_tensor_tensor(out=hid[:, n % 2, :], in0=bank_of(step)[:],
                                                  scalar=col("up_s", f), in1=silu[:, n % 2, :],
                                                  op0=ALU.mult, op1=ALU.mult), hid_ready)
                elif kind == "down" and step[3] == DPIECES - 1:
                    _, b, t, _ = step
                    n = b * TPB + t
                    wait_full(dve, ("down", b, t))
                    if n == 0:
                        dve.wait_ge(bc_in, 16)
                    if t == 0:
                        dve.wait_ge(x_biased, TPB * (b + 1))
                    emit(dve.tensor_tensor(tmp[:], bank_of(("down", b, t))[:], bc[:, DOWN_S, :],
                                           ALU.mult), down_read)
                    emit(dve.tensor_tensor(X[:, n, :], X[:, n, :], tmp[:], ALU.add))
                elif kind == "wo":
                    _, b, t = step
                    n = b * TPB + t
                    wait_full(dve, step)
                    dve.wait_ge(x_biased, TPB * (b + 1))
                    emit(dve.tensor_tensor(X[:, n, :], X[:, n, :], bank_of(step)[:], ALU.add), wo_added[b])
                elif kind == "u1":
                    dve.wait_ge(p_hi, step[1] + 1)
                    emit(dve.tensor_tensor(pl, bank_of(step)[:], ph.bitcast(F32), ALU.subtract), p_lo)
                elif kind == "hidden":
                    _, b, i = step
                    n = unit1(b, i)
                    K = rows_of(i)
                    key = ("hup", b, i)
                    dve.wait_ge(hid_lo, n - 1)
                    dve.wait_ge(silu_ready, n + 1)
                    wait_full(dve, key)
                    emit(dve.scalar_tensor_tensor(out=hid[0:K, n % 2, :], in0=bank_of(key)[0:K, :],
                                                  scalar=col("fb_up", i)[0:K, :],
                                                  in1=silu[0:K, n % 2, :],
                                                  op0=ALU.add, op1=ALU.mult), hid_ready)
                elif kind == "zcopy":
                    dve.wait_ge(z_hi, step[1] + 1)
                    emit(dve.tensor_tensor(zl, banks[RING][:], zh.bitcast(F32), ALU.subtract), z_lo)
                elif kind == "out":
                    _, b, t = step
                    n = b * TPB + t
                    dve.wait_ge(y_biased, n + 1)
                    wait_full(dve, ("attn", b, t))
                    emit(dve.tensor_tensor(X[:, n, :], X[:, n, :], bank_of(("attn", b, t))[:],
                                           ALU.add), out_ready)

        @block.gpsimd
        def _(pool):
            done = [0]

            def link(ins):
                done[0] += 1
                ins.then_inc(pool_chain, 1)
                pool.wait_ge(pool_chain, done[0])

            for step in order:
                kind = step[0]
                if kind == "tables":
                    pool.wait_ge(rot_seed, 1)
                    n = 1
                    while n < SEQ:
                        known, grown = rot[:, :, :, 1:n + 1], rot[:, :, :, n + 1:2 * n + 1]
                        part = rot_t[:, :, :, 0:n]
                        nth = lambda c: rot[:, :, c:c + 1, n:n + 1].to_broadcast([P, DEPTH, 2, n])
                        link(pool.tensor_tensor(grown, known, nth(0), ALU.mult))
                        link(pool.tensor_tensor(part, known, nth(1), ALU.mult))
                        link(pool.tensor_tensor(grown[:, :, 0, :], grown[:, :, 0, :], part[:, :, 1, :],
                                                ALU.subtract))
                        link(pool.tensor_tensor(grown[:, :, 1, :], grown[:, :, 1, :], part[:, :, 0, :],
                                                ALU.add))
                        n *= 2
                    pool.tensor_copy(rot[DIM:P, :, 0, :], rot[DIM:P, :, 1, :]).then_inc(tables_ready, 1)
                    pool.wait_ge(tables_ready, 1)
                elif kind == "xbias":
                    b = step[1]
                    pool.wait_ge(bc_in, 16)
                    for t in range(TPB):
                        n = b * TPB + t
                        pool.wait_ge(xn_ready, n + 1)
                        pool.tensor_tensor(X[:, n, :], X[:, n, :], bc[:, BOUT, :],
                                           ALU.add).then_inc(x_biased, 1)
                elif kind == "ybias":
                    b = step[1]
                    if b == 0:
                        link(pool.tensor_tensor(bc[:, BIAS1, :], bc[:, BIAS1, :], bc[:, BIAS2, :], ALU.add))
                    for t in range(TPB):
                        n = b * TPB + t
                        pool.wait_ge(xn_ready, NBLK * TPB + n + 1)
                        pool.tensor_tensor(X[:, n, :], X[:, n, :], bc[:, BIAS1, :],
                                           ALU.add).then_inc(y_biased, 1)
                elif kind == "up":
                    n = unit(step[1], step[2])
                    pool.wait_ge(hid_hi, n + 1)
                    pool.tensor_tensor(hidl[:, n % FT, :], hid[:, n % 2, :], hidh[:, n % FT, :],
                                       ALU.subtract).then_inc(hid_lo, 1)
                elif kind == "hidden":
                    n = unit1(step[1], step[2])
                    K = rows_of(step[2])
                    pool.wait_ge(hid_hi, n + 1)
                    pool.tensor_tensor(actl[0:K, n % 2, :], hid[0:K, n % 2, :],
                                       acth[0:K, n % 2, :].bitcast(F32), ALU.subtract).then_inc(hid_lo, 1)
                elif kind == "cast" and step[1:] in general:
                    n = general.index(step[1:])
                    c0, c1 = chunk_range(*step[1:])
                    hi, lo = split[step[1]]
                    pool.wait_ge(part_hi, n + 1)
                    pool.tensor_tensor(lo[:, c0:c1], stage[:, slot(step[1:]), 0:c1 - c0].bitcast(F32),
                                       hi[:, c0:c1].bitcast(F32), ALU.subtract).then_inc(part_lo, 1)


def kernel(**inputs):
    import numpy as np
    import concourse.bacc as bacc
    from concourse.bass_utils import run_bass_kernel_spmd

    a = {k: np.asarray(v) for k, v in inputs.items()}
    A = {k[8:]: v for k, v in a.items() if k.startswith("L0_attn_")}
    tern = {k[7:]: v for k, v in a.items() if k.startswith("L0_ffn_")}
    low = {k[7:]: v for k, v in a.items() if k.startswith("L1_ffn_")}

    def tiles(m, n):
        return np.ascontiguousarray(m.reshape(n, P).T)

    def both(m):
        return np.concatenate([m.T, m.T])

    def inter(m):
        padded = np.zeros(IT * P, m.dtype)
        padded[:INTER] = m
        return tiles(padded, IT)

    eye = np.eye(DIM, dtype=np.float32)
    parts = {
        "ident": np.eye(P, dtype=np.float32),
        "blockones": np.kron(np.eye(P // MB), np.ones((MB, MB))).astype(np.float32),
        "twoeye": np.concatenate([eye, eye]),
        "ones": np.ones((P, P), np.float32),
        "sign": np.repeat(np.array([[1.0], [-1.0]], np.float32), DIM, axis=0),
        "gate_s": tiles(tern["gate_s"], FT), "up_s": tiles(tern["up_s"], FT),
        "ln1_w": both(A["ln1_w"]), "ln1_b": both(A["ln1_b"]),
        "re": both(A["phz_re"]), "im": both(A["phz_im"]),
        "lc_p": np.concatenate([A["lc_re"].T, A["lc_im"].T]),
        "lc_q": np.concatenate([A["lc_im"].T, A["lc_re"].T]),
        "scl": both(A["sc_lin"]), "ln2_w": both(A["ln2_w"]), "ln2_b": both(A["ln2_b"]),
        "lnl_w": both(A["lnl_w"][None]), "lnl_b": both(A["lnl_b"][None]),
        "b1": A["b1"].reshape(DEPTH * FH, P).T,
        "fb_gate": inter(low["b1"][:INTER]), "fb_up": inter(low["b1"][INTER:]),
        "win": A["Win"].T.reshape(KT, P, DIM).transpose(1, 0, 2).reshape(P, KT * DIM),
        "w2": A["W2"].reshape(DEPTH, DIM, FH, P).transpose(3, 0, 2, 1).reshape(P, -1),
    }
    u2 = np.zeros((IT * P, RANK), np.float32)
    u2[:INTER] = low["U2"]

    def codes_in(m):
        return m.reshape(FT, P, KT, P).transpose(0, 3, 2, 1).reshape(FT, P, D)

    arrays = {
        "x": a["L0_attn_x"].reshape(NTOK // P, P, D),
        "gate": codes_in(tern["gate_t"]), "up": codes_in(tern["up_t"]),
        "down": tern["down_t"].T.reshape(FT, P, D),
        "mask": a["L1_attn_mask"].T.reshape(KT, P, D),
        "weight": a["L1_attn_weight"].T.reshape(KT, P, D),
        "v1": low["V1"],
        "u2": u2.reshape(IT, P, RANK).transpose(1, 0, 2).reshape(P, IT * RANK),
        "u1": low["U1"].reshape(KT, P, RANK).transpose(1, 0, 2).reshape(P, KT * RANK),
        "v2": low["V2"],
        "params": np.concatenate([parts[n] for n in COLS], axis=1),
        "wide64": np.concatenate([A["W1"].transpose(2, 0, 1).reshape(DIM, DEPTH * DFF), A["Wout"].T], axis=1),
        "rows": np.stack([tern["down_s"], A["bout"], a["L1_attn_bias"], low["b2"]]),
        "rows64": np.concatenate([A["b2"], A["bin"][None]])[None],
    }
    nc = bacc.Bacc("TRN2", target_bir_lowering=False, num_devices=1)
    feeds, args = {}, []
    for name, value in arrays.items():
        value = np.ascontiguousarray(value)
        feeds[f"in_{name}"] = value
        args.append(nc.dram_tensor(f"in_{name}", value.shape, mybir.dt.from_np(value.dtype),
                                   kind="ExternalInput").ap())
    out = nc.dram_tensor("out_x", (NTOK // P, P, D), F32, kind="ExternalOutput").ap()
    two_layers(nc, *args, out)
    result = run_bass_kernel_spmd(nc, [feeds], core_ids=[0])
    return result.results[0]["out_x"].reshape(4, SEQ, D)
```

```python
from contextlib import ExitStack

import concourse.bass as bass
from concourse import mybir

F32 = mybir.dt.float32
F32R = mybir.dt.float32r
F16 = mybir.dt.float16
I32 = mybir.dt.int32
ALU = mybir.AluOpType
ACT = mybir.ActivationFunctionType
AX = mybir.AxisListType

P = 128
NTOK, D = 1024, 512
NBLK = 2
BT = NTOK // NBLK
TPB = BT // P
KT = D // P
SEQ = 256
SPB = BT // SEQ
DEPTH, DIM, DFF = 4, 64, 256
FH = DFF // P
FF = 1792
FT = FF // P
INTER, RANK = 1376, 128
IT = -(-INTER // P)
MB = 32
EPS = 1e-5
SEED = 1597463007.0
NSTAGE = 6
RING = 6
DPIECES = 4

EARLY = (("ident", P), ("sign", 1), ("gate_s", FT), ("up_s", FT), ("re", DEPTH), ("im", DEPTH),
         ("lc_p", DEPTH), ("lc_q", DEPTH), ("scl", DEPTH), ("ln1_w", DEPTH), ("ln1_b", DEPTH),
         ("ln2_w", DEPTH), ("ln2_b", DEPTH), ("lnl_w", 1), ("lnl_b", 1), ("b1", DEPTH * FH),
         ("fb_gate", IT), ("fb_up", IT))
LATE = (("win", KT * DIM), ("w2", DEPTH * FH * DIM), ("twoeye", DIM), ("ones", P), ("blockones", P))


def columns(parts):
    at, n = {}, 0
    for name, width in parts:
        at[name] = n
        n += width
    return at, n


EARLY_AT, N_EARLY = columns(EARLY)
LATE_AT, N_LATE = columns(LATE)


def chunks_of(total):
    return [(c, min(c + D, total)) for c in range(0, total, D)]


V1_CHUNKS = chunks_of(2 * INTER)
U2_CHUNKS = chunks_of(IT * RANK)


def build_order():
    def ln_big(layer, b):
        return ([("stats", layer, b, t) for t in range(TPB)] + [("root", layer, b, 0, TPB)]
                + [("norm", layer, b, t) for t in range(TPB)])

    def chain(b):
        jobs = [(0, [("win", b), ("ln", b)]), (LN_SLOTS, [("scale", b)])]
        for l in range(DEPTH):
            jobs += [(1, [("t1", b, l)]), (1, [("scan", b, l)]), (SCAN_SLOTS, [("z", b, l), ("ln", b)]),
                     (LN_SLOTS, [("scale", b)]), (1, [("t3", b, l)]), (ACT_SLOTS, [("w1", b, l)]),
                     (ACT_SLOTS, [("w2", b, l), ("ln", b)]), (LN_SLOTS, [("scale", b)])]
        jobs += [(1, [("tf", b)]), (ACT_SLOTS, [("wo", b, 0), ("wo", b, 1)]),
                 (1, [("wo", b, 2), ("wo", b, 3)])]
        return jobs

    slots = []
    for b in range(NBLK):
        for f in range(FT):
            slots += [[("gate", b, f)], [("up", b, f)]]
        for t in range(TPB):
            slots += [[("down", b, t, q)] for q in range(DPIECES)]
    n_slots = len(slots)
    after = [[] for _ in slots]
    first_b = n_slots // 2
    up_at = lambda b, f: b * first_b + 2 * f + 1

    for f in range(FT):
        if f + 2 < FT:
            after[up_at(0, f) - 1].append(("cast", "gate", f + 2))
            after[up_at(0, f)].append(("cast", "up", f + 2))
        after[up_at(0, f)].append(("cast", "down", f))
    for i in range(POOL_GROWTHS, GROWTHS):
        after[3 * (i - POOL_GROWTHS)].append(("grow", i))
    after[3 * (GROWTHS - POOL_GROWTHS)].append(("lower",))
    pieces = ln_big(0, 1)
    for i, p in enumerate(pieces):
        after[1 + i // 2].append(p)
    for t in range(TPB):
        after[6 + t].append(("xt", 1, t))
    after[12].append(("xbias", 0))
    after[16].append(("xbias", 1))
    last = {}
    for b in range(NBLK):
        s = CHAIN_START[b]
        for distance, job in chain(b):
            s += distance
            after[int(s)] += job
        last[b] = int(s)
    for k in range(KT):
        after[first_b - 6 + k].append(("cast", "mask", k))
    after[first_b - 1].append(("maskones",))
    after[first_b + 1].append(("cast", "U1", 0))
    for i in range(len(V1_CHUNKS)):
        after[up_at(1, 2 * i + 1) + 1].append(("cast", "V1", i))
    for i in range(len(U2_CHUNKS)):
        after[up_at(1, 2 * i + 1) - 1].append(("cast", "U2", i))
    for k in range(KT):
        after[min(last[1] + 1 + k, n_slots - 1)].append(("cast", "w", k))

    order = [("seed",)]
    for t in range(TPB):
        order += [("stats", 0, 0, t), ("root", 0, 0, t, 1)]
        if t:
            order.append(("norm", 0, 0, t - 1))
        if t > 1:
            order.append(("cast", ("gate", "up")[t - 2], 0))
    order += [("norm", 0, 0, TPB - 1)] + [("xt", 0, t) for t in range(TPB)]
    order += [("cast", k, 1) for k in ("gate", "up")]
    order += [("grow", i) for i in range(POOL_GROWTHS)]
    ln1 = ln_big(1, 0)
    ln1_at = max(last[0], first_b - 1)
    for s in range(n_slots):
        order += slots[s] + after[s]
        k = s - ln1_at
        if 1 <= k <= 3:
            order += ln1[3 * (k - 1):3 * k]
        elif 4 <= k < 4 + TPB:
            order.append(("yt", 0, k - 4))
        if s - first_b - 2 * FT >= DPIECES and (s - first_b - 2 * FT) % DPIECES == 1:
            order.append(("stats", 1, 1, (s - first_b - 2 * FT) // DPIECES - 1))
    assert ln1_at + 4 + TPB <= n_slots and last[1] < n_slots
    order += [("u1", 0), ("stats", 1, 1, TPB - 1), ("cast", "V2", 0)]
    ln1 = ln_big(1, 1)[TPB:]
    for i in range(IT):
        order.append(("hidden", 0, i))
        if i < len(ln1):
            order.append(ln1[i])
        elif i < len(ln1) + TPB:
            order.append(("yt", 1, i - len(ln1)))
    order += [("attn", 0, 0), ("hidden_end", 0), ("attn", 0, 1), ("zcopy", 0), ("ybias", 0)]
    order += [("u1", 1), ("out", 0, 0), ("out", 0, 1), ("attn", 0, 2), ("out", 0, 2), ("attn", 0, 3),
              ("out", 0, 3)]
    order += [("hidden", 1, i) for i in range(IT)]
    order += [("attn", 1, 0), ("ybias", 1), ("hidden_end", 1), ("attn", 1, 1), ("zcopy", 1)]
    order += [("out", 1, 0), ("out", 1, 1), ("attn", 1, 2), ("out", 1, 2), ("attn", 1, 3), ("out", 1, 3)]
    return order


CHAIN_START = (4.0, 10.0)
LN_SLOTS, SCAN_SLOTS, ACT_SLOTS = 2.0, 2.2, 1.6
POOL_GROWTHS = 6
GROWTHS = SEQ.bit_length() - 1


def place_psum(order):
    where, turns, n = {}, [0] * (RING + 2), 0
    open_bank = None

    def take(key, bank=None):
        nonlocal n
        if bank is None:
            n += n % RING == open_bank
            bank = n % RING
            n += 1
        turns[bank] += 1
        where[key] = (bank, turns[bank])

    for step in order:
        kind = step[0]
        if kind in ("xt", "yt", "t1", "t3", "tf", "wo", "maskones", "gate", "up", "u1"):
            take(step)
        elif kind == "down":
            key = ("down", *step[1:3])
            if step[3] == 0:
                take(key)
            open_bank = where[key][0] if step[3] < DPIECES - 1 else None
        elif kind == "w1":
            for half in range(FH):
                take((*step, half))
        elif kind == "hidden":
            take(("hgate", *step[1:]))
            take(("hup", *step[1:]))
        elif kind == "attn":
            take(step, RING + 1 if step[2] == 0 else None)
        elif kind == "hidden_end":
            take(("zsum", step[1]), RING)
    return where


def two_layers(nc: bass.Bass, x, gate, up, down, mask, weight, v1, u2, u1, v2, params, params2, wide64,
               rows, rows64, out):
    order = build_order()
    psum_at = place_psum(order)
    casts = [s[1:] for s in order if s[0] == "cast"]
    ternary = [c for c in casts if c[0] in ("gate", "up", "down")]
    general = [c for c in casts if c[0] in ("U1", "V1", "U2", "w", "V2")]
    source = {"gate": gate, "up": up, "down": down, "mask": mask, "w": weight}

    with ExitStack() as ctx:
        def sb(name, shape, dt=F32, at=ctx):
            return at.enter_context(nc.sbuf_tensor(name, shape, dt))

        def sem(name):
            return ctx.enter_context(nc.semaphore(name))

        def overlay(first, second):
            size = lambda group: sum(w * (2 if dt == F16 else 4) for _, w, dt in group)
            small, large = sorted((first, second), key=size)
            with ExitStack() as s:
                tiles = {n: s.enter_context(nc.sbuf_tensor(n, [P, w], dt)) for n, w, dt in small}
            tiles |= {n: ctx.enter_context(nc.sbuf_tensor(n, [P, w], dt)) for n, w, dt in large}
            return tiles

        X = sb("X", [P, NTOK // P, D])
        XN = sb("XN", [P, TPB, D])
        stage = sb("stage", [P, NSTAGE, D], I32)
        early, late = sb("early", [P, N_EARLY]), sb("late", [P, N_LATE])
        w64 = sb("w64", [DIM, DEPTH * DFF + D])
        w1t = w64[:, 0:DEPTH * DFF].rearrange("p (l f) -> p l f", l=DEPTH)
        woutt = w64[:, DEPTH * DFF:]
        bc = sb("bc", [P, 4, D])
        row64 = sb("row64", [1, DEPTH + 1, DIM])
        r0 = overlay([("XT", KT * BT, F32), ("xh0", KT * BT, F16), ("xl0", KT * BT, F16)],
                     [("yh0", KT * BT, F32R), ("yl0", KT * BT, F32R)])
        xb1 = [sb(n, [P, KT, BT], F16) for n in ("xh1", "xl1")]
        r1 = overlay([("gatew", FT * D, F16), ("upw", FT * D, F16)],
                     [("V1h", FT * D // 2, F32R), ("V1l", FT * D // 2, F32R)])
        r2 = overlay([("hidh", FT * BT, F16), ("hidl", FT * BT, F16)],
                     [("yh1", KT * BT, F32R), ("yl1", KT * BT, F32R),
                      ("acth", 2 * BT, F32R), ("actl", 2 * BT, F32R)])
        r3 = overlay([("downw", FT * D, F16)],
                     [("V2h", D, F32R), ("V2l", D, F32R), ("ph", BT, F32R), ("pl", BT, F32R),
                      ("zh", BT, F32R), ("zl", BT, F32R)])
        U2h, U2l = sb("U2h", [P, IT * RANK], F32R), sb("U2l", [P, IT * RANK], F32R)
        mini = []
        for b in range(NBLK):
            mini += [(f"lno{b}", TPB * P, F32), (f"ymini{b}", BT, F32), (f"uscan{b}", BT, F32),
                     (f"yff{b}", FH * BT, F32)]
        r4 = overlay(mini + [("rot", DEPTH * 2 * (SEQ + 1), F32)],
                     [("Wh", KT * D, F32R), ("Wl", KT * D, F32R)])
        U1h, U1l = sb("U1h", [P, KT * RANK], F32R), sb("U1l", [P, KT * RANK], F32R)
        silu = sb("silu", [P, 2, BT])
        hid = sb("hid", [P, 2, BT])
        tmp = sb("tmp", [P, D])
        st = sb("st", [P, TPB, 6])
        mv = sb("mv", [P, TPB, 2])
        mvs = [sb(f"mvs{b}", [P, TPB, 2]) for b in range(NBLK)]
        var = [sb(f"var{i}", [P, TPB]) for i in range(NBLK + 1)]
        root = [sb(f"root{i}", [P, TPB]) for i in range(NBLK + 1)]
        cen = sb("cen", [P, TPB, DIM])
        powers = sb("powers", [P, 2, TPB])
        pz = sb("pz", [P, 8, DEPTH])
        scan0 = sb("scan0", [P, DEPTH])
        rad = sb("rad", [P, DEPTH])
        msum = sb("msum", [P, KT * D // MB])
        m01 = sb("m01", [P, KT * D // MB])

        tile = lambda group, name, a: group[name][:].rearrange("p (a n) -> p a n", a=a)
        XT = tile(r0, "XT", KT)
        xh = [tile(r0, "xh0", KT), xb1[0][:]]
        xl = [tile(r0, "xl0", KT), xb1[1][:]]
        yh = [tile(r0, "yh0", KT), tile(r2, "yh1", KT)]
        yl = [tile(r0, "yl0", KT), tile(r2, "yl1", KT)]
        codes = {"gate": tile(r1, "gatew", FT), "up": tile(r1, "upw", FT), "down": tile(r3, "downw", FT)}
        hidh, hidl = tile(r2, "hidh", FT), tile(r2, "hidl", FT)
        acth, actl = tile(r2, "acth", 2), tile(r2, "actl", 2)
        lno = [tile(r4, f"lno{b}", TPB) for b in range(NBLK)]
        ymini = [r4[f"ymini{b}"][:] for b in range(NBLK)]
        uscan = [r4[f"uscan{b}"][:] for b in range(NBLK)]
        yff = [tile(r4, f"yff{b}", FH) for b in range(NBLK)]
        rot_t = r4["yff0"][:].rearrange("p (l c t) -> p l c t", l=DEPTH, c=2)
        rot = r4["rot"][:].rearrange("p (l c t) -> p l c t", l=DEPTH, c=2)
        Wh, Wl = tile(r4, "Wh", KT), tile(r4, "Wl", KT)
        split = {"U1": (U1h[:], U1l[:]), "V1": (r1["V1h"][:], r1["V1l"][:]),
                 "U2": (U2h[:], U2l[:]), "V2": (r3["V2h"][:], r3["V2l"][:]),
                 "w": (r4["Wh"][:], r4["Wl"][:])}
        ph, pl, zh, zl = (r3[n][:] for n in ("ph", "pl", "zh", "zl"))

        def col(name, i=0, n=1):
            tile, at = (early, EARLY_AT[name]) if name in EARLY_AT else (late, LATE_AT[name])
            return tile[:, at + i:at + i + n]

        ident, twoeye = col("ident", 0, P), col("twoeye", 0, DIM)
        winT = col("win", 0, KT * DIM).rearrange("p (k d) -> p k d", k=KT)
        w2T = col("w2", 0, DEPTH * FH * DIM).rearrange("p (l h d) -> p l h d", l=DEPTH, h=FH)
        DOWN_S, BOUT, BIAS1, BIAS2 = range(4)

        banks = [ctx.enter_context(nc.psum_tensor(f"bank{i}", [P, D], F32)) for i in range(RING + 2)]
        h = [banks[RING + b][:, 0:TPB * DIM].rearrange("p (t d) -> p t d", t=TPB) for b in range(NBLK)]

        x_in = [sem(f"x_in{t}") for t in range(NTOK // P)]
        prm_in, late_in, w64_in, bc_in, row64_in = sem("prm_in"), sem("late_in"), sem("w64_in"), sem("bc_in"), sem("row64_in")
        stage_in = [sem(f"stage_in{i}") for i in range(NSTAGE)]
        full = [sem(f"psum_full{i}") for i in range(RING + 2)]
        dve_chain, pool_chain = sem("dve_chain"), sem("pool_chain")
        xn_ready = sem("xn_ready")
        xt_hi, xt_lo = sem("xt_hi"), sem("xt_lo")
        yt_hi, yt_lo = sem("yt_hi"), sem("yt_lo")
        x_biased, y_biased = sem("x_biased"), sem("y_biased")
        codes_ready = sem("codes_ready")
        part_hi, part_lo = sem("part_hi"), sem("part_lo")
        masked = sem("masked")
        mask_on = sem("mask_on")
        silu_ready = sem("silu_ready")
        hid_ready = sem("hid_ready")
        hid_hi, hid_lo = sem("hid_hi"), sem("hid_lo")
        h_full = [sem(f"h_full{b}") for b in range(NBLK)]
        ln_ready = [sem(f"ln_ready{b}") for b in range(NBLK)]
        y_ready = [sem(f"y_ready{b}") for b in range(NBLK)]
        z_ready = [sem(f"z_ready{b}") for b in range(NBLK)]
        ff_ready = [sem(f"ff_ready{b}") for b in range(NBLK)]
        size_ready, rad_ready = sem("size_ready"), sem("rad_ready")
        tables_ready = sem("tables_ready")
        p_hi, p_lo, z_hi, z_lo = sem("p_hi"), sem("p_lo"), sem("z_hi"), sem("z_lo")
        out_ready, out_done = sem("out_ready"), sem("out_done")
        down_read = sem("down_read")
        wo_added = [sem(f"wo_added{b}") for b in range(NBLK)]
        act_used = sem("act_used")
        var_ready = [sem(f"var_ready{i}") for i in range(NBLK + 1)]
        root_ready = [sem(f"root_ready{i}") for i in range(NBLK + 1)]

        def wait_full(eng, key):
            bank, turn = psum_at[key]
            eng.wait_ge(full[bank], turn)

        def released(key):
            kind, b, *rest = key if len(key) > 1 else (*key, 0)
            at = b * TPB + (rest[0] if rest else 0) + 1
            return {
                "xt": lambda: (xt_hi, at),
                "yt": lambda: (yt_lo, at),
                "t1": lambda: (y_ready[b], 2 * rest[0] + 1),
                "t3": lambda: (y_ready[b], 2 * rest[0] + 2),
                "tf": lambda: (y_ready[b], 2 * DEPTH + 1),
                "w1": lambda: (ff_ready[b], FH * rest[0] + rest[1] + 1),
                "wo": lambda: (wo_added[b], rest[0] + 1),
                "gate": lambda: (silu_ready, unit(b, rest[0]) + 1),
                "up": lambda: (hid_ready, unit(b, rest[0]) + 1),
                "down": lambda: (down_read, at),
                "maskones": lambda: (mask_on, 1),
                "u1": lambda: (p_lo, b + 1),
                "hgate": lambda: (silu_ready, unit1(b, rest[0]) + 1),
                "hup": lambda: (hid_ready, unit1(b, rest[0]) + 1),
                "zsum": lambda: (z_lo, b + 1),
                "attn": lambda: (out_ready, at),
            }[kind]()

        tenant = {v: k for k, v in psum_at.items()}

        def wait_bank(pe, key):
            bank, turn = psum_at[key]
            if turn > 1:
                pe.wait_ge(*released(tenant[bank, turn - 1]))

        def bank_of(key):
            return banks[psum_at[key][0]]

        def full_of(key):
            return full[psum_at[key][0]]

        def landed(eng, cast):
            n = casts.index(cast)
            eng.wait_ge(stage_in[n % NSTAGE], 16 * (n // NSTAGE + 1))

        def slot(cast):
            return casts.index(cast) % NSTAGE

        def chunk_range(kind, i):
            c0, c1 = {"V1": V1_CHUNKS, "U2": U2_CHUNKS}[kind][i] if kind in ("V1", "U2") else \
                (i * D, (i + 1) * D)
            return c0, c1

        def unit(b, f):
            return b * FT + f

        def unit1(b, i):
            return NBLK * FT + b * IT + i

        rows_of = lambda i: min(P, INTER - i * P)
        ln_count = 2 * DEPTH + 1

        def growth(i):
            n = 1 << i
            nth = lambda c: rot[:, :, c:c + 1, n:n + 1].to_broadcast([P, DEPTH, 2, n])
            return rot[:, :, :, 1:n + 1], rot[:, :, :, n + 1:2 * n + 1], rot_t[:, :, :, 0:n], nth

        block = ctx.enter_context(nc.Block())

        @block.sync
        def _(sp):
            sp.dma_start(X[:, 0, :], x[0]).then_inc(x_in[0], 16)
            sp.dma_start(early[:], params).then_inc(prm_in, 16)
            for t in range(1, TPB):
                sp.dma_start(X[:, t, :], x[t]).then_inc(x_in[t], 16)

            def load(n):
                kind, i = casts[n]
                if n >= NSTAGE:
                    before = casts[n - NSTAGE]
                    if before in ternary:
                        sp.wait_ge(codes_ready, ternary.index(before) + 1)
                    elif before in general:
                        sp.wait_ge(part_lo, general.index(before) + 1)
                    else:
                        sp.wait_ge(masked, before[1] + 1)
                if kind in ("V1", "U2"):
                    c0, c1 = chunk_range(kind, i)
                    src = (v1 if kind == "V1" else u2)[:, c0:c1]
                elif kind in ("U1", "V2"):
                    src, c0, c1 = (u1 if kind == "U1" else v2), 0, D
                else:
                    src, c0, c1 = source[kind][i], 0, D
                dst = stage[:, n % NSTAGE, 0:c1 - c0]
                if kind not in ("gate", "up", "down", "mask"):
                    dst = dst.bitcast(F32)
                sp.dma_start(dst, src).then_inc(stage_in[n % NSTAGE], 16)

            for n in range(4):
                load(n)
            sp.dma_start(late[:], params2).then_inc(late_in, 16)
            sp.dma_start(w64[:], wide64).then_inc(w64_in, 16)
            sp.dma_start(row64[:], rows64).then_inc(row64_in, 16)
            sp.dma_start(bc[:], rows.partition_broadcast(P)).then_inc(bc_in, 16)
            for t in range(TPB, 2 * TPB):
                sp.dma_start(X[:, t, :], x[t]).then_inc(x_in[t], 16)
            for n in range(4, len(casts)):
                load(n)
            for t in range(NTOK // P):
                sp.wait_ge(out_ready, t + 1)
                sp.dma_start(out[t], X[:, t, :]).then_inc(out_done, 16)
            sp.wait_ge(out_done, 16 * (NTOK // P))

        @block.tensor
        def _(pe):
            def transpose_tile(key, ready, count):
                wait_bank(pe, key)
                pe.wait_ge(ready, count)
                for k in range(KT):
                    mm = pe.transpose(bank_of(key)[:, k * P:(k + 1) * P],
                                      XN[:, key[2], k * P:(k + 1) * P], ident)
                mm.then_inc(full_of(key), 1)

            def three_passes(dst, lhs, rhs, first, last):
                pe.matmul(dst, lhs[0], rhs[0], start=first, stop=False)
                pe.matmul(dst, lhs[0], rhs[1], start=False, stop=False)
                return pe.matmul(dst, lhs[1], rhs[0], start=False, stop=last)

            def low_rank_down(b, i):
                n = unit1(b, i)
                pe.wait_ge(hid_lo, n + 1)
                if i == 0:
                    if b == 0:
                        pe.wait_ge(part_lo, general.index(("U2", 0)) + 1)
                        pe.wait_ge(ln_ready[0], ln_count)
                    else:
                        pe.wait_ge(z_lo, 1)
                if b == 0 and i * RANK // D > 0:
                    pe.wait_ge(part_lo, general.index(("U2", i * RANK // D)) + 1)
                K, c = rows_of(i), slice(i * RANK, (i + 1) * RANK)
                mm = three_passes(banks[RING][:], [w[0:K, c] for w in split["U2"]],
                                  [a[0:K, n % 2, :] for a in (acth, actl)], i == 0, i == IT - 1)
                return mm.then_inc(full[RING] if i == IT - 1 else act_used, 1)

            pe.wait_ge(prm_in, 16)
            for step in order:
                kind = step[0]
                if kind in ("xt", "yt"):
                    layer = 0 if kind == "xt" else 1
                    transpose_tile(step, xn_ready, (layer * NBLK + step[1]) * TPB + step[2] + 1)
                elif kind == "win":
                    b = step[1]
                    pe.wait_ge(xt_hi, TPB * (b + 1))
                    pe.wait_ge(row64_in, 16)
                    pe.wait_ge(late_in, 16)
                    for t in range(TPB):
                        for k in range(KT):
                            pe.matmul(h[b][:, t, :], XT[:, k, t * P:(t + 1) * P], winT[:, k, :],
                                      start=(t == 0 and k == 0), stop=False, skip_group_check=True)
                        mm = pe.matmul(h[b][:, t, :], col("ones", 0, P)[0:1, :], row64[0:1, DEPTH, :],
                                       start=False, stop=False, skip_group_check=True)
                    mm.then_inc(h_full[b], 1)
                elif kind in ("t1", "t3", "tf"):
                    b = step[1]
                    count = DEPTH * 2 + 1 if kind == "tf" else 2 * step[2] + (1 if kind == "t1" else 2)
                    wait_bank(pe, step)
                    pe.wait_ge(ln_ready[b], count)
                    w = P if kind == "t1" else DIM
                    for t in range(TPB):
                        mm = pe.transpose(bank_of(step)[0:w, t * P:(t + 1) * P], lno[b][:, t, 0:w], ident)
                    mm.then_inc(full_of(step), 1)
                elif kind == "z":
                    _, b, l = step
                    pe.wait_ge(z_ready[b], l + 1)
                    for t in range(TPB):
                        mm = pe.matmul(h[b][:, t, :], ymini[b][:, t * P:(t + 1) * P], twoeye,
                                       start=False, stop=False, skip_group_check=True)
                    mm.then_inc(h_full[b], 1)
                elif kind == "w1":
                    _, b, l = step
                    pe.wait_ge(y_ready[b], 2 * l + 2)
                    pe.wait_ge(w64_in, 16)
                    for half in range(FH):
                        key = (*step, half)
                        wait_bank(pe, key)
                        pe.matmul(bank_of(key)[:], w1t[:, l, half * P:(half + 1) * P], ymini[b][0:DIM, :],
                                  start=True, stop=True).then_inc(full_of(key), 1)
                elif kind == "w2":
                    _, b, l = step
                    pe.wait_ge(ff_ready[b], FH * (l + 1))
                    for t in range(TPB):
                        pe.matmul(h[b][:, t, :], col("ones", 0, P)[0:1, :], row64[0:1, l, :],
                                  start=False, stop=False, skip_group_check=True)
                        for half in range(FH):
                            mm = pe.matmul(h[b][:, t, :], yff[b][:, half, t * P:(t + 1) * P],
                                           w2T[:, l, half, :], start=False, stop=False,
                                           skip_group_check=True)
                    mm.then_inc(h_full[b], 1)
                elif kind == "wo":
                    _, b, t = step
                    wait_bank(pe, step)
                    pe.wait_ge(y_ready[b], 2 * DEPTH + 1)
                    pe.matmul(bank_of(step)[:], ymini[b][0:DIM, t * P:(t + 1) * P], woutt,
                              start=True, stop=True).then_inc(full_of(step), 1)
                elif kind in ("gate", "up"):
                    _, b, f = step
                    wait_bank(pe, step)
                    pe.wait_ge(codes_ready, ternary.index((kind, f)) + 1)
                    pe.wait_ge(xt_lo, TPB * (b + 1))
                    for k in range(KT):
                        w = codes[kind][:, f, k * P:(k + 1) * P]
                        pe.matmul(bank_of(step)[:], w, xh[b][:, k, :], start=(k == 0), stop=False)
                        mm = pe.matmul(bank_of(step)[:], w, xl[b][:, k, :], start=False, stop=(k == KT - 1))
                    mm.then_inc(full_of(step), 1)
                elif kind == "down":
                    _, b, t, q = step
                    key = ("down", b, t)
                    if q == 0:
                        wait_bank(pe, key)
                        if t == 0:
                            pe.wait_ge(codes_ready, len(ternary))
                    edges = [FT * i // DPIECES for i in range(DPIECES + 1)]
                    for f in range(edges[q], edges[q + 1]):
                        if t == 0:
                            pe.wait_ge(hid_lo, unit(b, f) + 1)
                        for part in (hidh, hidl):
                            mm = pe.matmul(bank_of(key)[:], part[:, f, t * P:(t + 1) * P],
                                           codes["down"][:, f, :], start=(f == 0 and part is hidh),
                                           stop=(f == FT - 1 and part is hidl))
                    if q == DPIECES - 1:
                        mm.then_inc(full_of(key), 1)
                elif kind == "maskones":
                    wait_bank(pe, step)
                    pe.wait_ge(masked, KT)
                    pe.matmul(bank_of(step)[:, 0:KT * D // MB], col("blockones", 0, P), msum[:],
                              start=True, stop=True).then_inc(full_of(step), 1)
                elif kind == "u1":
                    b = step[1]
                    wait_bank(pe, step)
                    pe.wait_ge(yt_lo, TPB * (b + 1))
                    pe.wait_ge(part_lo, general.index(("U1", 0)) + 1)
                    for k in range(KT):
                        c = slice(k * RANK, (k + 1) * RANK)
                        mm = three_passes(bank_of(step)[:], [w[:, c] for w in split["U1"]],
                                          [yh[b][:, k, :], yl[b][:, k, :]], k == 0, k == KT - 1)
                    mm.then_inc(full_of(step), 1)
                elif kind == "hidden":
                    _, b, i = step
                    if i == 0:
                        pe.wait_ge(p_lo, b + 1)
                    if b == 0:
                        pe.wait_ge(part_lo, general.index(("V1", (INTER + i * P + rows_of(i) - 1) // D)) + 1)
                    for key, off in ((("hgate", b, i), 0), (("hup", b, i), INTER)):
                        wait_bank(pe, key)
                        c = slice(off + i * P, off + i * P + rows_of(i))
                        three_passes(bank_of(key)[0:rows_of(i), :], [w[:, c] for w in split["V1"]],
                                     [ph, pl], True, True).then_inc(full_of(key), 1)
                    if i >= 2:
                        low_rank_down(b, i - 2)
                elif kind == "hidden_end":
                    b = step[1]
                    low_rank_down(b, IT - 2)
                    low_rank_down(b, IT - 1)
                elif kind == "attn":
                    _, b, t = step
                    wait_bank(pe, step)
                    if b == 0:
                        pe.wait_ge(part_lo, len(general))
                    if (b, t) == (0, 0):
                        pe.wait_ge(ln_ready[1], ln_count)
                    c = slice(t * P, (t + 1) * P)
                    for k in range(KT):
                        three_passes(bank_of(step)[:], [yh[b][:, k, c], yl[b][:, k, c]],
                                     [Wh[:, k, :], Wl[:, k, :]], k == 0, False)
                elif kind == "out":
                    _, b, t = step
                    pe.wait_ge(z_lo, b + 1)
                    c = slice(t * P, (t + 1) * P)
                    key = ("attn", b, t)
                    three_passes(bank_of(key)[:], [zh[:, c], zl[:, c]], split["V2"],
                                 False, True).then_inc(full_of(key), 1)

        @block.scalar
        def _(act):
            def hidden_hi(n):
                act.wait_ge(hid_ready, n + 1)
                if n < NBLK * FT:
                    if n == FT:
                        wait_full(act, ("down", 0, TPB - 1))
                    act.activation(hidh[:, n % FT, :], hid[:, n % 2, :], ACT.Copy).then_inc(hid_hi, 1)
                else:
                    b, i = divmod(n - NBLK * FT, IT)
                    K = rows_of(i)
                    if i >= 2:
                        act.wait_ge(act_used, b * (IT - 1) + i - 1)
                    act.activation(acth[0:K, n % 2, :], hid[0:K, n % 2, :], ACT.Copy).then_inc(hid_hi, 1)

            act.wait_ge(prm_in, 16)
            for step in order:
                kind = step[0]
                if kind == "xt":
                    _, b, t = step
                    if b == 1 and t == 0:
                        act.wait_ge(h_full[0], 1)
                        act.wait_ge(xt_lo, TPB)
                    wait_full(act, step)
                    src = bank_of(step)[:].rearrange("p (k n) -> p k n", k=KT)
                    c = slice(t * P, (t + 1) * P)
                    act.activation(xh[b][:, :, c], src, ACT.Copy)
                    act.activation(XT[:, :, c], src, ACT.Copy).then_inc(xt_hi, 1)
                elif kind == "seed":
                    act.wait_ge(size_ready, 1)
                    act.activation(rad[:], pz[:, 1, :], ACT.Tanh).then_inc(rad_ready, 1)
                elif kind == "yt":
                    _, b, t = step
                    wait_full(act, step)
                    src = bank_of(step)[:].rearrange("p (k n) -> p k n", k=KT)
                    act.activation(yh[b][:, :, t * P:(t + 1) * P], src, ACT.Copy).then_inc(yt_hi, 1)
                elif kind == "t1":
                    _, b, l = step
                    wait_full(act, step)
                    act.activation(ymini[b], bank_of(step)[:], ACT.Silu, bias=col("ln1_b", l),
                                   scale=col("ln1_w", l)).then_inc(y_ready[b], 1)
                elif kind in ("t3", "tf"):
                    b = step[1]
                    w, c = (col("ln2_w", step[2]), col("ln2_b", step[2])) if kind == "t3" else \
                        (col("lnl_w"), col("lnl_b"))
                    wait_full(act, step)
                    act.activation(ymini[b][0:DIM, :], bank_of(step)[0:DIM, :], ACT.Identity,
                                   bias=c[0:DIM, :], scale=w[0:DIM, :]).then_inc(y_ready[b], 1)
                elif kind == "w1":
                    _, b, l = step
                    for half in range(FH):
                        key = (*step, half)
                        wait_full(act, key)
                        act.activation(yff[b][:, half, :], bank_of(key)[:], ACT.Silu,
                                       bias=col("b1", l * FH + half)).then_inc(ff_ready[b], 1)
                elif kind == "gate":
                    _, b, f = step
                    n = unit(b, f)
                    if n >= 2:
                        act.wait_ge(hid_ready, n - 1)
                    wait_full(act, step)
                    act.activation(silu[:, n % 2, :], bank_of(step)[:], ACT.Silu,
                                   scale=col("gate_s", f)).then_inc(silu_ready, 1)
                    if f >= 1:
                        hidden_hi(n - 1)
                elif kind == "down" and step[2:] == (0, 0):
                    hidden_hi(unit(step[1], FT - 1))
                elif kind == "u1":
                    wait_full(act, step)
                    act.activation(ph, bank_of(step)[:], ACT.Copy).then_inc(p_hi, 1)
                elif kind == "hidden":
                    _, b, i = step
                    n = unit1(b, i)
                    K = rows_of(i)
                    act.wait_ge(hid_ready, n - 1)
                    wait_full(act, ("hgate", b, i))
                    act.activation(silu[0:K, n % 2, :], bank_of(("hgate", b, i))[0:K, :], ACT.Silu,
                                   bias=col("fb_gate", i)[0:K, :]).then_inc(silu_ready, 1)
                    if i >= 1:
                        hidden_hi(n - 1)
                elif kind == "hidden_end":
                    hidden_hi(unit1(step[1], IT - 1))
                elif kind == "zcopy":
                    wait_full(act, ("zsum", step[1]))
                    act.activation(zh, banks[RING][:], ACT.Copy).then_inc(z_hi, 1)

        @block.vector
        def _(dve):
            counts = {}

            def emit(ins, signal=dve_chain, hold=True):
                counts[id(signal)] = counts.get(id(signal), 0) + 1
                ins.then_inc(signal, 1)
                if hold:
                    dve.wait_ge(signal, counts[id(signal)])

            mini_norms = [0] * NBLK
            for step in order:
                kind = step[0]
                if kind == "stats":
                    _, layer, b, t = step
                    n = b * TPB + t
                    if layer == 0:
                        dve.wait_ge(x_in[n], 16)
                    emit(dve.bn_stats(st[:, t, :], X[:, n, :]))
                    emit(dve.bn_aggr(mv[:, t, :], st[:, t, :]))
                elif kind == "root":
                    t, n = step[3:]
                    emit(dve.tensor_scalar(var[NBLK][:, t:t + n], mv[:, t:t + n, 1], EPS, None, ALU.add),
                         var_ready[NBLK])
                elif kind == "norm":
                    _, layer, b, t = step
                    n = b * TPB + t
                    dve.wait_ge(root_ready[NBLK], t + 1 if (layer, b) == (0, 0) else
                                TPB + layer * NBLK + b)
                    before = layer * NBLK + b - 1
                    if before >= 0:
                        wait_full(dve, ("yt" if before >= NBLK else "xt", before % NBLK, t))
                    emit(dve.tensor_scalar(XN[:, t, :], X[:, n, :], mv[:, t, 0:1], root[NBLK][:, t:t + 1],
                                           ALU.subtract, ALU.mult), xn_ready)
                elif kind == "xt":
                    _, b, t = step
                    dve.wait_ge(xt_hi, b * TPB + t + 1)
                    c = slice(t * P, (t + 1) * P)
                    emit(dve.tensor_tensor(xl[b][:, :, c], XT[:, :, c], xh[b][:, :, c], ALU.subtract), xt_lo)
                elif kind == "yt":
                    _, b, t = step
                    dve.wait_ge(yt_hi, b * TPB + t + 1)
                    c = slice(t * P, (t + 1) * P)
                    src = bank_of(step)[:].rearrange("p (k n) -> p k n", k=KT)
                    emit(dve.tensor_tensor(yl[b][:, :, c], src, yh[b][:, :, c].bitcast(F32),
                                           ALU.subtract), yt_lo)
                elif kind == "grow" and step[1] >= POOL_GROWTHS:
                    if step[1] == POOL_GROWTHS:
                        dve.wait_ge(tables_ready, 1)
                    known, grown, part, nth = growth(step[1])
                    emit(dve.tensor_tensor(grown, known, nth(0), ALU.mult), hold=False)
                    emit(dve.tensor_tensor(part, known, nth(1), ALU.mult))
                    emit(dve.tensor_tensor(grown[:, :, 0, :], grown[:, :, 0, :], part[:, :, 1, :],
                                           ALU.subtract), hold=False)
                    emit(dve.tensor_tensor(grown[:, :, 1, :], grown[:, :, 1, :], part[:, :, 0, :],
                                           ALU.add))
                elif kind == "lower":
                    emit(dve.tensor_copy(rot[DIM:P, :, 0, :], rot[DIM:P, :, 1, :]))
                elif kind == "ln":
                    b = step[1]
                    k = mini_norms[b]
                    mini_norms[b] += 1
                    dve.wait_ge(h_full[b], k + 1)
                    for t in range(TPB):
                        emit(dve.bn_stats(st[:, t, :], h[b][:, t, :]), hold=t == TPB - 1)
                    for t in range(TPB):
                        emit(dve.bn_aggr(mvs[b][:, t, :], st[:, t, :]), hold=t == TPB - 1)
                    emit(dve.tensor_scalar(var[b][:], mvs[b][:, :, 1], EPS, None, ALU.add), var_ready[b])
                elif kind == "scale":
                    b = step[1]
                    k = mini_norms[b] - 1
                    mean = mvs[b][:, :, 0:1].to_broadcast([P, TPB, DIM])
                    emit(dve.tensor_tensor(cen[:], h[b], mean, ALU.subtract))
                    dve.wait_ge(root_ready[b], k + 1)
                    if k % 2 == 0 and k < 2 * DEPTH:
                        src = cen[:].unsqueeze(2).to_broadcast([P, TPB, 2, DIM])
                        dst = lno[b].rearrange("p t (c d) -> p t c d", c=2)
                        by = root[b][:].unsqueeze(2).unsqueeze(3).to_broadcast([P, TPB, 2, DIM])
                    else:
                        src, dst = cen[:], lno[b][:, :, 0:DIM]
                        by = root[b][:].unsqueeze(2).to_broadcast([P, TPB, DIM])
                    emit(dve.tensor_tensor(dst, src, by, ALU.mult), ln_ready[b])
                elif kind == "scan":
                    _, b, l = step
                    y = ymini[b].rearrange("p (s t) -> p s t", s=SPB)
                    u = uscan[b].rearrange("p (s t) -> p s t", s=SPB)
                    turn = rot[:, l, 0, 0:SEQ].unsqueeze(1).to_broadcast([P, SPB, SEQ])
                    if l == 0:
                        dve.wait_ge(rad_ready, 1)
                    dve.wait_ge(y_ready[b], 2 * l + 1)
                    emit(dve.tensor_tensor(y, y, turn, ALU.mult))
                    for s in range(SPB):
                        emit(dve.tensor_tensor_scan(u[:, s, :], rad[:, l:l + 1].to_broadcast([P, SEQ]),
                                                    y[:, s, :], scan0[:, l:l + 1], ALU.mult, ALU.add),
                             hold=s == SPB - 1)
                    emit(dve.scalar_tensor_tensor(out=y, in0=u, scalar=col("scl", l), in1=turn,
                                                  op0=ALU.mult, op1=ALU.mult), z_ready[b])
                elif kind == "cast":
                    _, what, i = step
                    landed(dve, step[1:])
                    c0, c1 = chunk_range(what, i)
                    src = stage[:, slot(step[1:]), 0:c1 - c0]
                    if what in codes:
                        emit(dve.tensor_copy(codes[what][:, i, :], src), codes_ready)
                    elif what == "mask":
                        nb = D // MB
                        emit(dve.tensor_reduce(msum[:, i * nb:(i + 1) * nb],
                                               src.rearrange("p (a n) -> p a n", n=MB), AX.X, ALU.add),
                             masked)
                    else:
                        src = src.bitcast(F32)
                        if what == "V1":
                            wait_full(dve, ("up", 1, 2 * i + 1))
                        if what == "V2":
                            wait_full(dve, ("down", 1, TPB - 1))
                        if what == "w":
                            if i == 0:
                                wait_full(dve, ("wo", 1, TPB - 1))
                            nb = D // MB
                            on = m01[:, i * nb:(i + 1) * nb].unsqueeze(2).to_broadcast([P, nb, MB])
                            blocks = src.rearrange("p (a n) -> p a n", n=MB)
                            emit(dve.tensor_tensor(blocks, blocks, on, ALU.mult))
                        hi = split[what][0]
                        emit(dve.tensor_copy(hi[:, c0:c1], src), part_hi)
                elif kind == "maskones":
                    wait_full(dve, step)
                    emit(dve.tensor_scalar(m01[:], bank_of(step)[:, 0:KT * D // MB], 0.0, None,
                                           ALU.is_gt), mask_on)
                elif kind == "up":
                    _, b, f = step
                    n = unit(b, f)
                    if n >= 2:
                        dve.wait_ge(hid_lo, n - 1)
                    dve.wait_ge(silu_ready, n + 1)
                    wait_full(dve, step)
                    emit(dve.scalar_tensor_tensor(out=hid[:, n % 2, :], in0=bank_of(step)[:],
                                                  scalar=col("up_s", f), in1=silu[:, n % 2, :],
                                                  op0=ALU.mult, op1=ALU.mult), hid_ready)
                elif kind == "down" and step[3] == DPIECES - 1:
                    _, b, t, _ = step
                    n = b * TPB + t
                    wait_full(dve, ("down", b, t))
                    if n == 0:
                        dve.wait_ge(bc_in, 16)
                    if t == 0:
                        dve.wait_ge(x_biased, TPB * (b + 1))
                    emit(dve.tensor_tensor(tmp[:], bank_of(("down", b, t))[:], bc[:, DOWN_S, :],
                                           ALU.mult), down_read)
                    emit(dve.tensor_tensor(X[:, n, :], X[:, n, :], tmp[:], ALU.add))
                elif kind == "wo":
                    _, b, t = step
                    n = b * TPB + t
                    wait_full(dve, step)
                    dve.wait_ge(x_biased, TPB * (b + 1))
                    emit(dve.tensor_tensor(X[:, n, :], X[:, n, :], bank_of(step)[:], ALU.add), wo_added[b])
                elif kind == "u1":
                    dve.wait_ge(p_hi, step[1] + 1)
                    emit(dve.tensor_tensor(pl, bank_of(step)[:], ph.bitcast(F32), ALU.subtract), p_lo)
                elif kind == "hidden":
                    _, b, i = step
                    n = unit1(b, i)
                    K = rows_of(i)
                    key = ("hup", b, i)
                    dve.wait_ge(hid_lo, n - 1)
                    dve.wait_ge(silu_ready, n + 1)
                    wait_full(dve, key)
                    emit(dve.scalar_tensor_tensor(out=hid[0:K, n % 2, :], in0=bank_of(key)[0:K, :],
                                                  scalar=col("fb_up", i)[0:K, :],
                                                  in1=silu[0:K, n % 2, :],
                                                  op0=ALU.add, op1=ALU.mult), hid_ready)
                elif kind == "zcopy":
                    dve.wait_ge(z_hi, step[1] + 1)
                    emit(dve.tensor_tensor(zl, banks[RING][:], zh.bitcast(F32), ALU.subtract), z_lo)
                elif kind == "out":
                    _, b, t = step
                    n = b * TPB + t
                    dve.wait_ge(y_biased, n + 1)
                    wait_full(dve, ("attn", b, t))
                    emit(dve.tensor_tensor(X[:, n, :], X[:, n, :], bank_of(("attn", b, t))[:],
                                           ALU.add), out_ready)

        @block.gpsimd
        def _(pool):
            done = [0]

            def link(ins):
                done[0] += 1
                ins.then_inc(pool_chain, 1)
                pool.wait_ge(pool_chain, done[0])

            link(pool.memset(powers[:, 0, :], -0.5))
            link(pool.memset(powers[:, 1, :], 0.5))
            rooted = [0] * NBLK + [0]

            def inverse_root(i, t=0, n=TPB):
                rooted[i] += 1
                pool.wait_ge(var_ready[i], rooted[i])
                pool.tensor_tensor(root[i][:, t:t + n], var[i][:, t:t + n], powers[:, 0, t:t + n],
                                   ALU.pow).then_inc(root_ready[i], 1)

            for step in order:
                kind = step[0]
                if kind == "seed":
                    re, im = col("re", 0, DEPTH), col("im", 0, DEPTH)
                    s2, size, inv, zero, re1, im1, c0, c1 = (pz[:, i, :] for i in range(8))
                    pool.wait_ge(prm_in, 16)
                    link(pool.tensor_tensor(s2, re, re, ALU.mult))
                    link(pool.tensor_tensor(c0, im, im, ALU.mult))
                    link(pool.tensor_tensor(s2, s2, c0, ALU.add))
                    pool.tensor_tensor(size, s2, powers[:, 1, :], ALU.pow).then_inc(size_ready, 1)
                elif kind == "grow" and step[1] == 0:
                    pool.wait_ge(size_ready, 1)
                    link(pool.tensor_scalar(zero, s2, 0.0, None, ALU.is_equal))
                    link(pool.tensor_tensor(re1, re, zero, ALU.add))
                    link(pool.tensor_tensor(zero, s2, zero, ALU.add))
                    link(pool.tensor_tensor(inv, zero, powers[:, 0, :], ALU.pow))
                    link(pool.tensor_scalar(im1, im, -1.0, None, ALU.mult))
                    link(pool.tensor_tensor(rot[:, :, 0, 1], re1, inv, ALU.mult))
                    link(pool.tensor_tensor(rot[:, :, 1, 1], im1, inv, ALU.mult))
                    link(pool.memset(rot[:, :, 0, 0:1], 1.0))
                    link(pool.memset(rot[:, :, 1, 0:1], 0.0))
                    link(pool.tensor_tensor(c0, rot[:, :, 0, 1], col("lc_p", 0, DEPTH), ALU.mult))
                    link(pool.tensor_scalar(c1, col("lc_q", 0, DEPTH), col("sign"), None, ALU.mult))
                    link(pool.tensor_tensor(c1, rot[:, :, 1, 1], c1, ALU.mult))
                    link(pool.tensor_tensor(scan0[:], c0, c1, ALU.add))
                if kind == "grow" and step[1] < POOL_GROWTHS:
                    known, grown, part, nth = growth(step[1])
                    link(pool.tensor_tensor(grown, known, nth(0), ALU.mult))
                    link(pool.tensor_tensor(part, known, nth(1), ALU.mult))
                    link(pool.tensor_tensor(grown[:, :, 0, :], grown[:, :, 0, :], part[:, :, 1, :],
                                            ALU.subtract))
                    last = pool.tensor_tensor(grown[:, :, 1, :], grown[:, :, 1, :], part[:, :, 0, :],
                                              ALU.add)
                    if step[1] == POOL_GROWTHS - 1:
                        last.then_inc(tables_ready, 1)
                    else:
                        link(last)
                elif kind == "root":
                    inverse_root(NBLK, *step[3:])
                elif kind == "ln":
                    inverse_root(step[1])
                elif kind == "xbias":
                    b = step[1]
                    pool.wait_ge(bc_in, 16)
                    for t in range(TPB):
                        n = b * TPB + t
                        pool.wait_ge(xn_ready, n + 1)
                        pool.tensor_tensor(X[:, n, :], X[:, n, :], bc[:, BOUT, :],
                                           ALU.add).then_inc(x_biased, 1)
                elif kind == "ybias":
                    b = step[1]
                    if b == 0:
                        link(pool.tensor_tensor(bc[:, BIAS1, :], bc[:, BIAS1, :], bc[:, BIAS2, :], ALU.add))
                    for t in range(TPB):
                        n = b * TPB + t
                        pool.wait_ge(xn_ready, NBLK * TPB + n + 1)
                        pool.tensor_tensor(X[:, n, :], X[:, n, :], bc[:, BIAS1, :],
                                           ALU.add).then_inc(y_biased, 1)
                elif kind == "up":
                    n = unit(step[1], step[2])
                    pool.wait_ge(hid_hi, n + 1)
                    pool.tensor_tensor(hidl[:, n % FT, :], hid[:, n % 2, :], hidh[:, n % FT, :],
                                       ALU.subtract).then_inc(hid_lo, 1)
                elif kind == "hidden":
                    n = unit1(step[1], step[2])
                    K = rows_of(step[2])
                    pool.wait_ge(hid_hi, n + 1)
                    pool.tensor_tensor(actl[0:K, n % 2, :], hid[0:K, n % 2, :],
                                       acth[0:K, n % 2, :].bitcast(F32), ALU.subtract).then_inc(hid_lo, 1)
                elif kind == "cast" and step[1:] in general:
                    n = general.index(step[1:])
                    c0, c1 = chunk_range(*step[1:])
                    hi, lo = split[step[1]]
                    pool.wait_ge(part_hi, n + 1)
                    pool.tensor_tensor(lo[:, c0:c1], stage[:, slot(step[1:]), 0:c1 - c0].bitcast(F32),
                                       hi[:, c0:c1].bitcast(F32), ALU.subtract).then_inc(part_lo, 1)


def kernel(**inputs):
    import numpy as np
    import concourse.bacc as bacc
    from concourse.bass_utils import run_bass_kernel_spmd

    a = {k: np.asarray(v) for k, v in inputs.items()}
    A = {k[8:]: v for k, v in a.items() if k.startswith("L0_attn_")}
    tern = {k[7:]: v for k, v in a.items() if k.startswith("L0_ffn_")}
    low = {k[7:]: v for k, v in a.items() if k.startswith("L1_ffn_")}

    def tiles(m, n):
        return np.ascontiguousarray(m.reshape(n, P).T)

    def both(m):
        return np.concatenate([m.T, m.T])

    def inter(m):
        padded = np.zeros(IT * P, m.dtype)
        padded[:INTER] = m
        return tiles(padded, IT)

    eye = np.eye(DIM, dtype=np.float32)
    parts = {
        "ident": np.eye(P, dtype=np.float32),
        "blockones": np.kron(np.eye(P // MB), np.ones((MB, MB))).astype(np.float32),
        "twoeye": np.concatenate([eye, eye]),
        "ones": np.ones((P, P), np.float32),
        "sign": np.repeat(np.array([[1.0], [-1.0]], np.float32), DIM, axis=0),
        "gate_s": tiles(tern["gate_s"], FT), "up_s": tiles(tern["up_s"], FT),
        "ln1_w": both(A["ln1_w"]), "ln1_b": both(A["ln1_b"]),
        "re": both(A["phz_re"]), "im": both(A["phz_im"]),
        "lc_p": np.concatenate([A["lc_re"].T, A["lc_im"].T]),
        "lc_q": np.concatenate([A["lc_im"].T, A["lc_re"].T]),
        "scl": both(A["sc_lin"]), "ln2_w": both(A["ln2_w"]), "ln2_b": both(A["ln2_b"]),
        "lnl_w": both(A["lnl_w"][None]), "lnl_b": both(A["lnl_b"][None]),
        "b1": A["b1"].reshape(DEPTH * FH, P).T,
        "fb_gate": inter(low["b1"][:INTER]), "fb_up": inter(low["b1"][INTER:]),
        "win": A["Win"].T.reshape(KT, P, DIM).transpose(1, 0, 2).reshape(P, KT * DIM),
        "w2": A["W2"].reshape(DEPTH, DIM, FH, P).transpose(3, 0, 2, 1).reshape(P, -1),
    }
    u2 = np.zeros((IT * P, RANK), np.float32)
    u2[:INTER] = low["U2"]

    def codes_in(m):
        return m.reshape(FT, P, KT, P).transpose(0, 3, 2, 1).reshape(FT, P, D)

    arrays = {
        "x": a["L0_attn_x"].reshape(NTOK // P, P, D),
        "gate": codes_in(tern["gate_t"]), "up": codes_in(tern["up_t"]),
        "down": tern["down_t"].T.reshape(FT, P, D),
        "mask": a["L1_attn_mask"].T.reshape(KT, P, D),
        "weight": a["L1_attn_weight"].T.reshape(KT, P, D),
        "v1": low["V1"],
        "u2": u2.reshape(IT, P, RANK).transpose(1, 0, 2).reshape(P, IT * RANK),
        "u1": low["U1"].reshape(KT, P, RANK).transpose(1, 0, 2).reshape(P, KT * RANK),
        "v2": low["V2"],
        "params": np.concatenate([parts[n] for n, _ in EARLY], axis=1),
        "params2": np.concatenate([parts[n] for n, _ in LATE], axis=1),
        "wide64": np.concatenate([A["W1"].transpose(2, 0, 1).reshape(DIM, DEPTH * DFF), A["Wout"].T], axis=1),
        "rows": np.stack([tern["down_s"], A["bout"], a["L1_attn_bias"], low["b2"]]),
        "rows64": np.concatenate([A["b2"], A["bin"][None]])[None],
    }
    nc = bacc.Bacc("TRN2", target_bir_lowering=False, num_devices=1)
    feeds, args = {}, []
    for name, value in arrays.items():
        value = np.ascontiguousarray(value)
        feeds[f"in_{name}"] = value
        args.append(nc.dram_tensor(f"in_{name}", value.shape, mybir.dt.from_np(value.dtype),
                                   kind="ExternalInput").ap())
    out = nc.dram_tensor("out_x", (NTOK // P, P, D), F32, kind="ExternalOutput").ap()
    two_layers(nc, *args, out)
    result = run_bass_kernel_spmd(nc, [feeds], core_ids=[0])
    return result.results[0]["out_x"].reshape(4, SEQ, D)
```

```python
from contextlib import ExitStack

import concourse.bass as bass
from concourse import mybir

F32 = mybir.dt.float32
F32R = mybir.dt.float32r
F16 = mybir.dt.float16
I32 = mybir.dt.int32
ALU = mybir.AluOpType
ACT = mybir.ActivationFunctionType
AX = mybir.AxisListType

P = 128
NTOK, D = 1024, 512
NBLK = 2
BT = NTOK // NBLK
TPB = BT // P
KT = D // P
SEQ = 256
SPB = BT // SEQ
DEPTH, DIM, DFF = 4, 64, 256
FH = DFF // P
FF = 1792
FT = FF // P
INTER, RANK = 1376, 128
IT = -(-INTER // P)
MB = 32
EPS = 1e-5
NSTAGE = 6
UNITS = 3
RING = 6
DPIECES = 4

EARLY = (("ident", P), ("sign", 1), ("gate_s", FT), ("up_s", FT), ("re", DEPTH), ("im", DEPTH),
         ("lc_p", DEPTH), ("lc_q", DEPTH), ("scl", DEPTH), ("ln1_w", DEPTH), ("ln1_b", DEPTH),
         ("ln2_w", DEPTH), ("ln2_b", DEPTH), ("lnl_w", 1), ("lnl_b", 1), ("b1", DEPTH * FH),
         ("fb_gate", IT), ("fb_up", IT))
LATE = (("win", KT * DIM), ("w2", DEPTH * FH * DIM), ("twoeye", DIM), ("blockones", P))


def columns(parts):
    at, n = {}, 0
    for name, width in parts:
        at[name] = n
        n += width
    return at, n


EARLY_AT, N_EARLY = columns(EARLY)
LATE_AT, N_LATE = columns(LATE)


def chunks_of(total):
    return [(c, min(c + D, total)) for c in range(0, total, D)]


V1_CHUNKS = chunks_of(2 * INTER)
U2_CHUNKS = chunks_of(IT * RANK)


def build_order():
    def ln_big(layer, b):
        return ([("stats", layer, b, t) for t in range(TPB)] + [("root", layer, b, 0, TPB)]
                + [("norm", layer, b, t) for t in range(TPB)])

    def chain(b):
        jobs = [(0, [("win", b), ("ln", b)]), (LN_SLOTS, [("scale", b)])]
        for l in range(DEPTH):
            jobs += [(1, [("t1", b, l)]), (1, [("scan", b, l)]), (SCAN_SLOTS, [("z", b, l), ("ln", b)]),
                     (LN_SLOTS, [("scale", b)]), (1, [("t3", b, l)]), (1, [("low", b)]),
                     (LOW_SLOTS, [("w1", b, l)]), (ACT_SLOTS, [("w2", b, l), ("ln", b)]),
                     (LN_SLOTS, [("scale", b)])]
        jobs += [(1, [("tf", b)]), (1, [("low", b)]), (LOW_SLOTS, [("wo", b, 0), ("wo", b, 1)]),
                 (1, [("wo", b, 2), ("wo", b, 3)])]
        return jobs

    slots = []
    for b in range(NBLK):
        for f in range(FT):
            slots += [[("gate", b, f)], [("up", b, f)]]
        for t in range(TPB):
            slots += [[("down", b, t, q)] for q in range(DPIECES)]
    n_slots = len(slots)
    after = [[] for _ in slots]
    first_b = n_slots // 2
    up_at = lambda b, f: b * first_b + 2 * f + 1

    for f in range(FT):
        if f + 2 < FT:
            after[up_at(0, f) - 1].append(("cast", "gate", f + 2))
            after[up_at(0, f)].append(("cast", "up", f + 2))
        after[up_at(0, f)].append(("cast", "down", f))
    for at, step in zip(LN_AT, ln_big(0, 1)):
        after[at].append(step)
    for i in range(GROWTHS):
        for part in range(4):
            after[GROW_AT[i] + (part if i == GROWTHS - 1 else 0)].append(("grow", i, part))
    after[GROW_AT[-1] + 3].append(("lower",))
    for t in range(TPB):
        after[XT_AT + XT_STEP * t].append(("xt", 1, t))
    for b in range(NBLK):
        after[XBIAS_AT[b]].append(("xbias", b))
    for i in range(DEPTH * DFF // D):
        after[W1_AT + i].append(("cast", "W1", i))
    after[WOUT_AT].append(("cast", "Wout", 0))
    last = {}
    for b in range(NBLK):
        s = CHAIN_START[b]
        for distance, job in chain(b):
            s += distance
            after[int(s)] += job
        last[b] = int(s)
    for k in range(KT):
        after[first_b - 6 + k].append(("cast", "mask", k))
    after[first_b - 1].append(("maskones",))
    after[first_b + 1].append(("cast", "U1", 0))
    for i in range(len(V1_CHUNKS)):
        after[up_at(1, 2 * i + 1) + 1].append(("cast", "V1", i))
    for i in range(len(U2_CHUNKS)):
        after[up_at(1, FT - 1) + 1 + i].append(("cast", "U2", i))
    for k in range(KT):
        after[last[1] - WMASK_BEFORE + k].append(("wmask", k))
        after[min(last[1] + 1 + k, n_slots - 1)].append(("cast", "w", k))

    placed = [step for slot in after for step in slot]
    assert placed.index(("lower",)) < placed.index(("scan", 0, 0))

    order = [("seed",)]
    for t in range(TPB + 3):
        if t < TPB:
            order += [("stats", 0, 0, t), ("root", 0, 0, t, 1)]
        if 1 <= t <= TPB:
            order.append(("norm", 0, 0, t - 1))
        if 2 <= t <= TPB + 1:
            order.append(("xt", 0, t - 2))
        if 2 <= t <= 3:
            order.append(("cast", ("gate", "up")[t - 2], 0))
        if 3 <= t:
            order.append(("first", t - 3))
    order += [("cast", k, 1) for k in ("gate", "up")] + [("rows",)]
    ln1 = ln_big(1, 0)
    ln1_at = last[0] + LN1_AFTER
    stats_done = 0
    for s in range(n_slots):
        order += slots[s] + after[s]
        if s == n_slots - U1_BEFORE_END:
            order.append(("u1", 0))
        k = s - ln1_at
        if 1 <= k <= 3:
            order += ln1[3 * (k - 1):3 * k]
        elif 4 <= k < 4 + TPB:
            order.append(("yt", 0, k - 4))
        if s >= last[1] and first_b + 2 * FT + DPIECES * (stats_done + 1) < s:
            order.append(("stats", 1, 1, stats_done))
            stats_done += 1
    assert ln1_at + 3 + TPB <= n_slots - U1_BEFORE_END and last[1] <= n_slots - U1_BEFORE_END
    order += [("stats", 1, 1, t) for t in range(stats_done, TPB)] + [("cast", "V2", 0)]
    ln1 = ln_big(1, 1)[TPB:]
    for i in range(IT):
        order.append(("hidden", 0, i))
        if i == FILL_AT:
            order.append(("attn", 0, 0))
        if i in YBIAS_AT[0]:
            order.append(("ybias", 0, YBIAS_AT[0].index(i)))
        if i < len(ln1):
            order.append(ln1[i])
        elif i < len(ln1) + TPB:
            order.append(("yt", 1, i - len(ln1)))
    order += [("attn", 0, 1), ("hidden_end", 0), ("attn", 0, 2), ("zcopy", 0)]
    order += [("u1", 1), ("out", 0, 0), ("out", 0, 1), ("attn", 0, 3), ("out", 0, 2), ("out", 0, 3)]
    for i in range(IT):
        order.append(("hidden", 1, i))
        if i == FILL_AT:
            order.append(("attn", 1, 0))
        if i in YBIAS_AT[1]:
            order.append(("ybias", 1, YBIAS_AT[1].index(i)))
    order += [("attn", 1, 1), ("hidden_end", 1), ("attn", 1, 2), ("zcopy", 1)]
    order += [("attn", 1, 3), ("out", 1, 0), ("out", 1, 1), ("out", 1, 2), ("out", 1, 3)]
    return order


CHAIN_START = (3, 12)
LN_SLOTS, SCAN_SLOTS = 2, 3.3
LOW_SLOTS, ACT_SLOTS = 2, 2.6
LN_AT = (1, 2, 3, 3, 3, 5, 5, 6, 8)
XT_AT, XT_STEP = 5, 2
GROWTHS = SEQ.bit_length() - 1
POOL_GROWTHS = 6
GROW_AT = (0, 0, 0, 0, 0, 0, 3, 4)
W1_AT, WOUT_AT = 6, 31
XBIAS_AT = (12, 16)
ACT_UPS = 6
LN1_AFTER = 2
WMASK_BEFORE = 4
U1_BEFORE_END = 4
FILL_AT = 1
LAG = 3
YBIAS_AT = ((4, 5, 6, 7), (1, 3, 5, 7))


def cast_by_act(kind, i):
    return kind == "down" or i == 0 or (kind == "up" and 1 < i < ACT_UPS)


def place_psum(order):
    where, turns, n = {}, [0] * (RING + 2), 0
    open_bank = None

    def take(key, bank=None):
        nonlocal n
        if bank is None:
            n += n % RING == open_bank
            bank = n % RING
            n += 1
        turns[bank] += 1
        where[key] = (bank, turns[bank])

    for f in ("gate", "up"):
        take((f, 0, 0))
    for step in order:
        kind = step[0]
        if step[1:] == (0, 0) and kind in ("gate", "up"):
            continue
        if kind in ("xt", "yt", "t1", "t3", "tf", "wo", "maskones", "gate", "up", "u1"):
            take(step)
        elif kind == "down":
            key = ("down", *step[1:3])
            if step[3] == 0:
                take(key)
            open_bank = where[key][0] if step[3] < DPIECES - 1 else None
        elif kind == "w1":
            for half in range(FH):
                take((*step, half))
        elif kind == "hidden":
            take(("hgate", *step[1:]))
            take(("hup", *step[1:]))
        elif kind == "attn":
            take(step, RING + 1 if step[2] == 0 else None)
        elif kind == "hidden_end":
            take(("zsum", step[1]), RING)
    return where


def two_layers(nc: bass.Bass, x, gate, up, down, mask, weight, v1, u2, u1, v2, params, params2, wide64,
               rows, rows64, out):
    order = build_order()
    psum_at = place_psum(order)
    casts = [s[1:] for s in order if s[0] == "cast"]
    ternary = {e: [c for c in casts if c[0] in ("gate", "up", "down") and (cast_by_act(*c) == (e == "act"))]
               for e in ("act", "dve")}
    general = [c for c in casts if c[0] in ("U1", "V1", "U2", "w", "V2", "W1", "Wout")]
    source = {"gate": gate, "up": up, "down": down, "mask": mask, "w": weight}

    with ExitStack() as ctx:
        def sb(name, shape, dt=F32, at=ctx):
            return at.enter_context(nc.sbuf_tensor(name, shape, dt))

        def sem(name):
            return ctx.enter_context(nc.semaphore(name))

        def overlay(first, second):
            size = lambda group: sum(w * (2 if dt == F16 else 4) for _, w, dt in group)
            small, large = sorted((first, second), key=size)
            with ExitStack() as s:
                tiles = {n: s.enter_context(nc.sbuf_tensor(n, [P, w], dt)) for n, w, dt in small}
            tiles |= {n: ctx.enter_context(nc.sbuf_tensor(n, [P, w], dt)) for n, w, dt in large}
            return tiles

        X = sb("X", [P, NTOK // P, D])
        XN = sb("XN", [P, TPB, D])
        stage = sb("stage", [P, NSTAGE, D], I32)
        early, late = sb("early", [P, N_EARLY]), sb("late", [P, N_LATE])
        W1h, W1l = sb("W1h", [P, DEPTH * DFF], F32R), sb("W1l", [DIM, DEPTH * DFF], F32R)
        Wouth, Woutl = sb("Wouth", [P, D], F32R), sb("Woutl", [DIM, D], F32R)
        onesr = sb("onesr", [1, P], F32R)
        bc = sb("bc", [P, 2, D])
        rowh, rowl = (sb(n, [1, DEPTH + 1, DIM], F32R) for n in ("rowh", "rowl"))
        r0 = overlay([("XT", KT * BT, F32), ("xh0", KT * BT, F16), ("xl0", KT * BT, F16)],
                     [("yh0", KT * BT, F32R), ("yl0", KT * BT, F32R)])
        r5 = overlay([("xh1", KT * BT, F16), ("xl1", KT * BT, F16)], [("U2h", IT * RANK, F32R)])
        r6 = overlay([(f"uscan{b}", BT, F32) for b in range(NBLK)],
                     [(f"xs{b}", BT, F32R) for b in range(NBLK)])
        r1 = overlay([("gatew", FT * D, F16), ("upw", FT * D, F16)],
                     [("V1h", FT * D // 2, F32R), ("V1l", FT * D // 2, F32R)])
        r2 = overlay([("hidh", FT * BT, F16), ("hidl", FT * BT, F16)],
                     [("yh1", KT * BT, F32R), ("yl1", KT * BT, F32R),
                      ("acth", UNITS * BT, F32R), ("actl", UNITS * BT, F32R)])
        r3 = overlay([("downw", FT * D, F16)],
                     [("V2h", D, F32R), ("V2l", D, F32R), ("zh", BT, F32R), ("zl", BT, F32R),
                      ("bias", 2 * D, F32)])
        U2l = sb("U2l", [P, IT * RANK], F32R)
        mini = []
        for b in range(NBLK):
            mini += [(f"lno{b}", TPB * P, F32), (f"ymini{b}", BT, F32),
                     (f"yff{b}", FH * BT, F32)]
        r4 = overlay(mini + [("rot", DEPTH * 2 * (SEQ + 1), F32)],
                     [("Wh", KT * D, F32R), ("Wl", KT * D, F32R)])
        U1h, U1l = sb("U1h", [P, KT * RANK], F32R), sb("U1l", [P, KT * RANK], F32R)
        silu = sb("silu", [P, UNITS, BT])
        hid = sb("hid", [P, UNITS, BT])
        tmp = sb("tmp", [P, D])
        st = sb("st", [P, TPB, 6])
        mv = sb("mv", [P, TPB, 2])
        mvs = [sb(f"mvs{b}", [P, TPB, 2]) for b in range(NBLK)]
        var = [sb(f"var{i}", [P, TPB]) for i in range(NBLK + 1)]
        root = [sb(f"root{i}", [P, TPB]) for i in range(NBLK + 1)]
        cen = sb("cen", [P, TPB, DIM])
        powers = sb("powers", [P, 2, TPB])
        pz = sb("pz", [P, 8, DEPTH])
        scan0 = sb("scan0", [P, DEPTH])
        rad = sb("rad", [P, DEPTH])
        msum = sb("msum", [P, KT * D // MB])
        m01 = sb("m01", [P, KT * D // MB])

        tile = lambda group, name, a: group[name][:].rearrange("p (a n) -> p a n", a=a)
        XT = tile(r0, "XT", KT)
        xh = [tile(r0, "xh0", KT), tile(r5, "xh1", KT)]
        xl = [tile(r0, "xl0", KT), tile(r5, "xl1", KT)]
        yh = [tile(r0, "yh0", KT), tile(r2, "yh1", KT)]
        yl = [tile(r0, "yl0", KT), tile(r2, "yl1", KT)]
        codes = {"gate": tile(r1, "gatew", FT), "up": tile(r1, "upw", FT), "down": tile(r3, "downw", FT)}
        hidh, hidl = tile(r2, "hidh", FT), tile(r2, "hidl", FT)
        acth, actl = tile(r2, "acth", UNITS), tile(r2, "actl", UNITS)
        lno = [tile(r4, f"lno{b}", TPB) for b in range(NBLK)]
        ymini = [r4[f"ymini{b}"][:] for b in range(NBLK)]
        uscan = [r6[f"uscan{b}"][:] for b in range(NBLK)]
        xs = [r6[f"xs{b}"][:] for b in range(NBLK)]
        yff = [tile(r4, f"yff{b}", FH) for b in range(NBLK)]
        rot_t = r4["yff0"][:].rearrange("p (l c t) -> p l c t", l=DEPTH, c=2)
        rot = r4["rot"][:].rearrange("p (l c t) -> p l c t", l=DEPTH, c=2)
        Wh, Wl = tile(r4, "Wh", KT), tile(r4, "Wl", KT)
        split = {"U1": (U1h[:], U1l[:]), "V1": (r1["V1h"][:], r1["V1l"][:]),
                 "U2": (r5["U2h"][:], U2l[:]), "V2": (r3["V2h"][:], r3["V2l"][:]),
                 "w": (r4["Wh"][:], r4["Wl"][:]), "W1": (W1h[:], W1l[:]), "Wout": (Wouth[:], Woutl[:])}
        ph, pl = xs
        zh, zl = (r3[n][:] for n in ("zh", "zl"))

        def col(name, i=0, n=1):
            tile, at = (early, EARLY_AT[name]) if name in EARLY_AT else (late, LATE_AT[name])
            return tile[:, at + i:at + i + n]

        ident, twoeye = col("ident", 0, P), col("twoeye", 0, DIM)
        winT = col("win", 0, KT * DIM).rearrange("p (k d) -> p k d", k=KT)
        w2T = col("w2", 0, DEPTH * FH * DIM).rearrange("p (l h d) -> p l h d", l=DEPTH, h=FH)
        DOWN_S, BOUT = range(2)
        bias = tile(r3, "bias", 2)

        banks = [ctx.enter_context(nc.psum_tensor(f"bank{i}", [P, D], F32)) for i in range(RING + 2)]
        h = [banks[RING + b][:, 0:TPB * DIM].rearrange("p (t d) -> p t d", t=TPB) for b in range(NBLK)]

        x_in = [sem(f"x_in{t}") for t in range(NTOK // P)]
        prm_in, late_in, bc_in, row64_in = sem("prm_in"), sem("late_in"), sem("bc_in"), sem("row64_in")
        bias_in = sem("bias_in")
        stage_in = [sem(f"stage_in{i}") for i in range(NSTAGE)]
        full = [sem(f"psum_full{i}") for i in range(RING + 2)]
        dve_chain, pool_chain = sem("dve_chain"), sem("pool_chain")
        xn_ready = sem("xn_ready")
        xt_hi, xt_lo = sem("xt_hi"), sem("xt_lo")
        yt_hi, yt_lo = sem("yt_hi"), sem("yt_lo")
        x_biased, y_biased = sem("x_biased"), sem("y_biased")
        codes_ready = {"act": sem("codes_act"), "dve": sem("codes_dve")}
        part_hi, part_lo = sem("part_hi"), sem("part_lo")
        masked = sem("masked")
        mask_on = sem("mask_on")
        w_masked = sem("w_masked")
        silu_ready = sem("silu_ready")
        hid_ready = sem("hid_ready")
        hid_hi, hid_lo = sem("hid_hi"), sem("hid_lo")
        h_full = [sem(f"h_full{b}") for b in range(NBLK)]
        ln_ready = [sem(f"ln_ready{b}") for b in range(NBLK)]
        y_ready = [sem(f"y_ready{b}") for b in range(NBLK)]
        z_ready = [sem(f"z_ready{b}") for b in range(NBLK)]
        ff_ready = [sem(f"ff_ready{b}") for b in range(NBLK)]
        size_ready, rad_ready = sem("size_ready"), sem("rad_ready")
        tables_ready = sem("tables_ready")
        p_hi, p_lo, z_hi, z_lo = sem("p_hi"), sem("p_lo"), sem("z_hi"), sem("z_lo")
        out_ready, out_done = sem("out_ready"), sem("out_done")
        down_read = sem("down_read")
        wo_added = [sem(f"wo_added{b}") for b in range(NBLK)]
        act_used = sem("act_used")
        low_ready = [sem(f"low_ready{b}") for b in range(NBLK)]
        row_ready = sem("row_ready")
        var_ready = [sem(f"var_ready{i}") for i in range(NBLK + 1)]
        root_ready = [sem(f"root_ready{i}") for i in range(NBLK + 1)]

        def wait_full(eng, key):
            bank, turn = psum_at[key]
            eng.wait_ge(full[bank], turn)

        def released(key):
            kind, b, *rest = key if len(key) > 1 else (*key, 0)
            at = b * TPB + (rest[0] if rest else 0) + 1
            return {
                "xt": lambda: (xt_hi, at),
                "yt": lambda: (yt_lo, at),
                "t1": lambda: (y_ready[b], 2 * rest[0] + 1),
                "t3": lambda: (y_ready[b], 2 * rest[0] + 2),
                "tf": lambda: (y_ready[b], 2 * DEPTH + 1),
                "w1": lambda: (ff_ready[b], FH * rest[0] + rest[1] + 1),
                "wo": lambda: (wo_added[b], rest[0] + 1),
                "gate": lambda: (silu_ready, unit(b, rest[0]) + 1),
                "up": lambda: (hid_ready, unit(b, rest[0]) + 1),
                "down": lambda: (down_read, at),
                "maskones": lambda: (mask_on, 1),
                "u1": lambda: (p_lo, b + 1),
                "hgate": lambda: (silu_ready, unit1(b, rest[0]) + 1),
                "hup": lambda: (hid_ready, unit1(b, rest[0]) + 1),
                "zsum": lambda: (z_lo, b + 1),
                "attn": lambda: (out_ready, at),
            }[kind]()

        tenant = {v: k for k, v in psum_at.items()}

        def wait_bank(pe, key):
            bank, turn = psum_at[key]
            if turn > 1:
                pe.wait_ge(*released(tenant[bank, turn - 1]))

        def bank_of(key):
            return banks[psum_at[key][0]]

        def full_of(key):
            return full[psum_at[key][0]]

        def landed(eng, cast):
            n = casts.index(cast)
            eng.wait_ge(stage_in[n % NSTAGE], 16 * (n // NSTAGE + 1))

        def wait_codes(eng, *cast):
            by = "act" if cast in ternary["act"] else "dve"
            eng.wait_ge(codes_ready[by], ternary[by].index(cast) + 1)

        def slot(cast):
            return casts.index(cast) % NSTAGE

        def chunk_range(kind, i):
            c0, c1 = {"V1": V1_CHUNKS, "U2": U2_CHUNKS}[kind][i] if kind in ("V1", "U2") else \
                (i * D, (i + 1) * D)
            return c0, c1

        def unit(b, f):
            return b * FT + f

        def unit1(b, i):
            return NBLK * FT + b * IT + i

        rows_of = lambda i: min(P, INTER - i * P)
        ln_count = 2 * DEPTH + 1

        def growth(eng, i, part):
            n = 1 << i
            known, grown, other = rot[:, :, :, 1:n + 1], rot[:, :, :, n + 1:2 * n + 1], rot_t[:, :, :, 0:n]
            if part < 2:
                nth = rot[:, :, part:part + 1, n:n + 1].to_broadcast([P, DEPTH, 2, n])
                return eng.tensor_tensor(other if part else grown, known, nth, ALU.mult)
            c = part - 2
            return eng.tensor_tensor(grown[:, :, c, :], grown[:, :, c, :], other[:, :, 1 - c, :],
                                     ALU.add if c else ALU.subtract)

        block = ctx.enter_context(nc.Block())

        @block.sync
        def _(sp):
            sp.dma_start(X[:, 0, :], x[0]).then_inc(x_in[0], 16)
            sp.dma_start(early[:], params).then_inc(prm_in, 16)
            def load(n):
                kind, i = casts[n]
                if n >= NSTAGE:
                    before = casts[n - NSTAGE]
                    if before[0] in codes:
                        wait_codes(sp, *before)
                    elif before in general:
                        sp.wait_ge(part_lo, general.index(before) + 1)
                    else:
                        sp.wait_ge(masked, before[1] + 1)
                if kind in ("V1", "U2", "W1", "Wout"):
                    c0, c1 = chunk_range(kind, i)
                    at = DEPTH * DFF if kind == "Wout" else 0
                    src = {"V1": v1, "U2": u2}.get(kind, wide64)[:, at + c0:at + c1]
                elif kind in ("U1", "V2"):
                    src, c0, c1 = (u1 if kind == "U1" else v2), 0, D
                else:
                    src, c0, c1 = source[kind][i], 0, D
                dst = stage[:, n % NSTAGE, 0:c1 - c0]
                if kind not in ("gate", "up", "down", "mask"):
                    dst = dst.bitcast(F32)
                sp.dma_start(dst, src).then_inc(stage_in[n % NSTAGE], 16)

            for t in range(1, TPB):
                sp.dma_start(X[:, t, :], x[t]).then_inc(x_in[t], 16)
            for n in range(4):
                load(n)
            sp.dma_start(tmp[0:1, 0:(DEPTH + 1) * DIM], rows64).then_inc(row64_in, 16)
            sp.dma_start(late[:], params2).then_inc(late_in, 16)
            for t in range(TPB, 2 * TPB):
                sp.dma_start(X[:, t, :], x[t]).then_inc(x_in[t], 16)
            for n in range(4, 12):
                load(n)
            sp.dma_start(bc[:], rows[0:2].partition_broadcast(P)).then_inc(bc_in, 16)
            for n in range(12, len(casts)):
                load(n)
            wait_full(sp, ("down", 1, TPB - 1))
            sp.dma_start(bias, rows[2:4].partition_broadcast(P)).then_inc(bias_in, 16)
            for t in range(NTOK // P):
                sp.wait_ge(out_ready, t + 1)
                sp.dma_start(out[t], X[:, t, :]).then_inc(out_done, 16)
            sp.wait_ge(out_done, 16 * (NTOK // P))

        @block.tensor
        def _(pe):
            def transpose_tile(key, ready, count):
                wait_bank(pe, key)
                pe.wait_ge(ready, count)
                for k in range(KT):
                    mm = pe.transpose(bank_of(key)[:, k * P:(k + 1) * P],
                                      XN[:, key[2], k * P:(k + 1) * P], ident)
                mm.then_inc(full_of(key), 1)

            def three_passes(dst, lhs, rhs, first, last):
                pe.matmul(dst, lhs[0], rhs[0], start=first, stop=False)
                pe.matmul(dst, lhs[0], rhs[1], start=False, stop=False)
                return pe.matmul(dst, lhs[1], rhs[0], start=False, stop=last)

            def low_rank_down(b, i):
                n = unit1(b, i)
                pe.wait_ge(hid_lo, n + 1)
                if i == 0:
                    if b == 0:
                        pe.wait_ge(part_lo, general.index(("U2", 0)) + 1)
                        pe.wait_ge(ln_ready[0], ln_count)
                    else:
                        pe.wait_ge(z_lo, 1)
                if b == 0 and i * RANK // D > 0:
                    pe.wait_ge(part_lo, general.index(("U2", i * RANK // D)) + 1)
                K, c = rows_of(i), slice(i * RANK, (i + 1) * RANK)
                mm = three_passes(banks[RING][:], [w[0:K, c] for w in split["U2"]],
                                  [a[0:K, n % UNITS, :] for a in (acth, actl)], i == 0, i == IT - 1)
                return mm.then_inc(full[RING] if i == IT - 1 else act_used, 1)

            def add_row(b, i, first):
                for part in (rowh, rowl):
                    pe.matmul(banks[RING + b][:, 0:TPB * DIM], onesr[:],
                              part[0:1, i:i + 1, :].to_broadcast([1, TPB, DIM]),
                              start=first and part is rowh, stop=False, skip_group_check=True)

            def gate_up(key, c, f):
                kind, b = key[0:2]
                for k in range(KT):
                    w = codes[kind][:, f, k * P:(k + 1) * P]
                    pe.matmul(bank_of(key)[:, c], w, xh[b][:, k, c], start=(k == 0), stop=False)
                    mm = pe.matmul(bank_of(key)[:, c], w, xl[b][:, k, c], start=False, stop=(k == KT - 1))
                return mm

            pe.wait_ge(prm_in, 16)
            for step in order:
                kind = step[0]
                if kind in ("xt", "yt"):
                    layer = 0 if kind == "xt" else 1
                    transpose_tile(step, xn_ready, (layer * NBLK + step[1]) * TPB + step[2] + 1)
                elif kind == "win":
                    b = step[1]
                    pe.wait_ge(xt_hi, TPB * (b + 1))
                    pe.wait_ge(late_in, 16)
                    pe.wait_ge(row_ready, 1)
                    add_row(b, DEPTH, True)
                    for t in range(TPB):
                        for k in range(KT):
                            mm = pe.matmul(h[b][:, t, :], XT[:, k, t * P:(t + 1) * P], winT[:, k, :],
                                           start=False, stop=False, skip_group_check=True)
                    mm.then_inc(h_full[b], 1)
                elif kind in ("t1", "t3", "tf"):
                    b = step[1]
                    count = DEPTH * 2 + 1 if kind == "tf" else 2 * step[2] + (1 if kind == "t1" else 2)
                    wait_bank(pe, step)
                    pe.wait_ge(ln_ready[b], count)
                    for t in range(TPB):
                        mm = pe.transpose(bank_of(step)[:, t * P:(t + 1) * P], lno[b][:, t, :], ident)
                    mm.then_inc(full_of(step), 1)
                elif kind == "z":
                    _, b, l = step
                    pe.wait_ge(z_ready[b], l + 1)
                    for t in range(TPB):
                        mm = pe.matmul(h[b][:, t, :], ymini[b][:, t * P:(t + 1) * P], twoeye,
                                       start=False, stop=False, skip_group_check=True)
                    mm.then_inc(h_full[b], 1)
                elif kind == "w1":
                    _, b, l = step
                    pe.wait_ge(low_ready[b], l + 1)
                    pe.wait_ge(part_lo, general.index(("W1", ((l + 1) * DFF - 1) // D)) + 1)
                    for half in range(FH):
                        key = (*step, half)
                        wait_bank(pe, key)
                        c = slice(l * DFF + half * P, l * DFF + (half + 1) * P)
                        pe.matmul(bank_of(key)[:], W1h[:, c], xs[b], start=True, stop=False)
                        pe.matmul(bank_of(key)[:], W1l[:, c], xs[b][0:DIM, :], start=False,
                                  stop=True).then_inc(full_of(key), 1)
                elif kind == "w2":
                    _, b, l = step
                    pe.wait_ge(ff_ready[b], FH * (l + 1))
                    add_row(b, l, False)
                    for t in range(TPB):
                        for half in range(FH):
                            mm = pe.matmul(h[b][:, t, :], yff[b][:, half, t * P:(t + 1) * P],
                                           w2T[:, l, half, :], start=False, stop=False,
                                           skip_group_check=True)
                    mm.then_inc(h_full[b], 1)
                elif kind == "wo":
                    _, b, t = step
                    wait_bank(pe, step)
                    pe.wait_ge(low_ready[b], DEPTH + 1)
                    pe.wait_ge(part_lo, general.index(("Wout", 0)) + 1)
                    c = slice(t * P, (t + 1) * P)
                    pe.matmul(bank_of(step)[:], xs[b][:, c], Wouth[:], start=True, stop=False)
                    pe.matmul(bank_of(step)[:], xs[b][0:DIM, c], Woutl[:], start=False,
                              stop=True).then_inc(full_of(step), 1)
                elif kind == "first":
                    t = step[1]
                    pe.wait_ge(xt_lo, t + 1)
                    for kind in ("gate", "up"):
                        wait_codes(pe, kind, 0)
                        mm = gate_up((kind, 0, 0), slice(t * P, (t + 1) * P), 0)
                        if t == TPB - 1:
                            mm.then_inc(full_of((kind, 0, 0)), 1)
                elif kind in ("gate", "up") and step[1:] != (0, 0):
                    _, b, f = step
                    wait_bank(pe, step)
                    wait_codes(pe, kind, f)
                    pe.wait_ge(xt_lo, TPB * (b + 1))
                    gate_up(step, slice(0, BT), f).then_inc(full_of(step), 1)
                elif kind == "down":
                    _, b, t, q = step
                    key = ("down", b, t)
                    if q == 0:
                        wait_bank(pe, key)
                        if t == 0:
                            for by in codes_ready:
                                pe.wait_ge(codes_ready[by], len(ternary[by]))
                    edges = [FT * i // DPIECES for i in range(DPIECES + 1)]
                    for f in range(edges[q], edges[q + 1]):
                        if t == 0:
                            pe.wait_ge(hid_lo, unit(b, f) + 1)
                        for part in (hidh, hidl):
                            mm = pe.matmul(bank_of(key)[:], part[:, f, t * P:(t + 1) * P],
                                           codes["down"][:, f, :], start=(f == 0 and part is hidh),
                                           stop=(f == FT - 1 and part is hidl))
                    if q == DPIECES - 1:
                        mm.then_inc(full_of(key), 1)
                elif kind == "maskones":
                    wait_bank(pe, step)
                    pe.wait_ge(masked, KT)
                    pe.matmul(bank_of(step)[:, 0:KT * D // MB], col("blockones", 0, P), msum[:],
                              start=True, stop=True).then_inc(full_of(step), 1)
                elif kind == "u1":
                    b = step[1]
                    wait_bank(pe, step)
                    pe.wait_ge(yt_lo, TPB * (b + 1))
                    pe.wait_ge(part_lo, general.index(("U1", 0)) + 1)
                    for k in range(KT):
                        c = slice(k * RANK, (k + 1) * RANK)
                        mm = three_passes(bank_of(step)[:], [w[:, c] for w in split["U1"]],
                                          [yh[b][:, k, :], yl[b][:, k, :]], k == 0, k == KT - 1)
                    mm.then_inc(full_of(step), 1)
                elif kind == "hidden":
                    _, b, i = step
                    if i == 0:
                        pe.wait_ge(p_lo, b + 1)
                    if b == 0:
                        pe.wait_ge(part_lo, general.index(("V1", (INTER + i * P + rows_of(i) - 1) // D)) + 1)
                    for key, off in ((("hgate", b, i), 0), (("hup", b, i), INTER)):
                        wait_bank(pe, key)
                        c = slice(off + i * P, off + i * P + rows_of(i))
                        three_passes(bank_of(key)[0:rows_of(i), :], [w[:, c] for w in split["V1"]],
                                     [ph, pl], True, True).then_inc(full_of(key), 1)
                    if i >= LAG:
                        low_rank_down(b, i - LAG)
                elif kind == "hidden_end":
                    b = step[1]
                    for i in range(IT - LAG, IT):
                        low_rank_down(b, i)
                elif kind == "attn":
                    _, b, t = step
                    wait_bank(pe, step)
                    if b == 0:
                        pe.wait_ge(part_lo, general.index(("w", KT - 1)) + 1)
                    if (b, t) == (0, 0):
                        pe.wait_ge(ln_ready[1], ln_count)
                    c = slice(t * P, (t + 1) * P)
                    for k in range(KT):
                        three_passes(bank_of(step)[:], [yh[b][:, k, c], yl[b][:, k, c]],
                                     [Wh[:, k, :], Wl[:, k, :]], k == 0, False)
                elif kind == "out":
                    _, b, t = step
                    pe.wait_ge(z_lo, b + 1)
                    pe.wait_ge(part_lo, general.index(("V2", 0)) + 1)
                    c = slice(t * P, (t + 1) * P)
                    key = ("attn", b, t)
                    three_passes(bank_of(key)[:], [zh[:, c], zl[:, c]], split["V2"],
                                 False, True).then_inc(full_of(key), 1)

        @block.scalar
        def _(act):
            def hidden_hi(n):
                act.wait_ge(hid_ready, n + 1)
                if n < NBLK * FT:
                    if n == FT:
                        wait_full(act, ("down", 0, TPB - 1))
                    act.activation(hidh[:, n % FT, :], hid[:, n % UNITS, :], ACT.Copy).then_inc(hid_hi, 1)
                else:
                    b, i = divmod(n - NBLK * FT, IT)
                    K = rows_of(i)
                    if i >= UNITS:
                        act.wait_ge(act_used, b * (IT - 1) + i - UNITS + 1)
                    act.activation(acth[0:K, n % UNITS, :], hid[0:K, n % UNITS, :],
                                   ACT.Copy).then_inc(hid_hi, 1)

            act.wait_ge(prm_in, 16)
            for step in order:
                kind = step[0]
                if kind == "xt":
                    _, b, t = step
                    if b == 1 and t == 0:
                        act.wait_ge(h_full[0], 1)
                        act.wait_ge(xt_lo, TPB)
                    wait_full(act, step)
                    src = bank_of(step)[:].rearrange("p (k n) -> p k n", k=KT)
                    c = slice(t * P, (t + 1) * P)
                    act.activation(xh[b][:, :, c], src, ACT.Copy)
                    act.activation(XT[:, :, c], src, ACT.Copy).then_inc(xt_hi, 1)
                elif kind == "cast" and step[1:] in ternary["act"]:
                    _, what, i = step
                    landed(act, step[1:])
                    act.activation(codes[what][:, i, :], stage[:, slot(step[1:]), :],
                                   ACT.Copy).then_inc(codes_ready["act"], 1)
                elif kind == "seed":
                    act.wait_ge(size_ready, 1)
                    act.activation(rad[:], pz[:, 1, :], ACT.Tanh).then_inc(rad_ready, 1)
                elif kind == "yt":
                    _, b, t = step
                    wait_full(act, step)
                    src = bank_of(step)[:].rearrange("p (k n) -> p k n", k=KT)
                    act.activation(yh[b][:, :, t * P:(t + 1) * P], src, ACT.Copy).then_inc(yt_hi, 1)
                elif kind == "t1":
                    _, b, l = step
                    wait_full(act, step)
                    act.activation(ymini[b], bank_of(step)[:], ACT.Silu, bias=col("ln1_b", l),
                                   scale=col("ln1_w", l)).then_inc(y_ready[b], 1)
                elif kind in ("t3", "tf"):
                    b = step[1]
                    w, c = (col("ln2_w", step[2]), col("ln2_b", step[2])) if kind == "t3" else \
                        (col("lnl_w"), col("lnl_b"))
                    wait_full(act, step)
                    act.activation(xs[b], bank_of(step)[:], ACT.Identity, bias=c, scale=w)
                    act.activation(ymini[b][DIM:P, :], bank_of(step)[DIM:P, :], ACT.Identity,
                                   bias=c[DIM:P, :], scale=w[DIM:P, :]).then_inc(y_ready[b], 1)
                elif kind == "w1":
                    _, b, l = step
                    for half in range(FH):
                        key = (*step, half)
                        wait_full(act, key)
                        act.activation(yff[b][:, half, :], bank_of(key)[:], ACT.Silu,
                                       bias=col("b1", l * FH + half)).then_inc(ff_ready[b], 1)
                elif kind == "gate":
                    _, b, f = step
                    n = unit(b, f)
                    if n >= UNITS:
                        act.wait_ge(hid_ready, n - UNITS + 1)
                    wait_full(act, step)
                    act.activation(silu[:, n % UNITS, :], bank_of(step)[:], ACT.Silu,
                                   scale=col("gate_s", f)).then_inc(silu_ready, 1)
                    if f >= 1:
                        hidden_hi(n - 1)
                elif kind == "down" and step[2:] == (0, 0):
                    hidden_hi(unit(step[1], FT - 1))
                elif kind == "u1":
                    wait_full(act, step)
                    act.activation(ph, bank_of(step)[:], ACT.Copy).then_inc(p_hi, 1)
                elif kind == "hidden":
                    _, b, i = step
                    n = unit1(b, i)
                    K = rows_of(i)
                    act.wait_ge(hid_ready, n - UNITS + 1)
                    wait_full(act, ("hgate", b, i))
                    act.activation(silu[0:K, n % UNITS, :], bank_of(("hgate", b, i))[0:K, :], ACT.Silu,
                                   bias=col("fb_gate", i)[0:K, :]).then_inc(silu_ready, 1)
                    if i >= 1:
                        hidden_hi(n - 1)
                elif kind == "hidden_end":
                    hidden_hi(unit1(step[1], IT - 1))
                elif kind == "zcopy":
                    wait_full(act, ("zsum", step[1]))
                    act.activation(zh, banks[RING][:], ACT.Copy).then_inc(z_hi, 1)

        @block.vector
        def _(dve):
            counts = {}

            def emit(ins, signal=dve_chain, hold=True):
                counts[id(signal)] = counts.get(id(signal), 0) + 1
                ins.then_inc(signal, 1)
                if hold:
                    dve.wait_ge(signal, counts[id(signal)])

            mini_norms = [0] * NBLK
            lows = [0] * NBLK
            for step in order:
                kind = step[0]
                if kind == "stats":
                    _, layer, b, t = step
                    n = b * TPB + t
                    if layer == 0:
                        dve.wait_ge(x_in[n], 16)
                    emit(dve.bn_stats(st[:, t, :], X[:, n, :]))
                    emit(dve.bn_aggr(mv[:, t, :], st[:, t, :]))
                elif kind == "root":
                    t, n = step[3:]
                    emit(dve.tensor_scalar(var[NBLK][:, t:t + n], mv[:, t:t + n, 1], EPS, None, ALU.add),
                         var_ready[NBLK])
                elif kind == "norm":
                    _, layer, b, t = step
                    n = b * TPB + t
                    dve.wait_ge(root_ready[NBLK], t + 1 if (layer, b) == (0, 0) else
                                TPB + layer * NBLK + b)
                    before = layer * NBLK + b - 1
                    if before >= 0:
                        wait_full(dve, ("yt" if before >= NBLK else "xt", before % NBLK, t))
                    emit(dve.tensor_scalar(XN[:, t, :], X[:, n, :], mv[:, t, 0:1], root[NBLK][:, t:t + 1],
                                           ALU.subtract, ALU.mult), xn_ready)
                elif kind == "xt":
                    _, b, t = step
                    dve.wait_ge(xt_hi, b * TPB + t + 1)
                    c = slice(t * P, (t + 1) * P)
                    emit(dve.tensor_tensor(xl[b][:, :, c], XT[:, :, c], xh[b][:, :, c], ALU.subtract), xt_lo)
                elif kind == "yt":
                    _, b, t = step
                    dve.wait_ge(yt_hi, b * TPB + t + 1)
                    c = slice(t * P, (t + 1) * P)
                    src = bank_of(step)[:].rearrange("p (k n) -> p k n", k=KT)
                    emit(dve.tensor_tensor(yl[b][:, :, c], src, yh[b][:, :, c].bitcast(F32),
                                           ALU.subtract), yt_lo)
                elif kind == "grow" and step[1] >= POOL_GROWTHS:
                    if step[1:] == (POOL_GROWTHS, 0):
                        dve.wait_ge(tables_ready, 1)
                    emit(growth(dve, *step[1:]), hold=step[2] % 2 == 1)
                elif kind == "rows":
                    n = (DEPTH + 1) * DIM
                    raw = tmp[0:1, 0:n].rearrange("p (l d) -> p l d", d=DIM)
                    dve.wait_ge(row64_in, 16)
                    emit(dve.tensor_copy(rowh[:], raw))
                    emit(dve.tensor_tensor(rowl[:], raw, rowh[:].bitcast(F32), ALU.subtract), hold=False)
                    emit(dve.memset(onesr[:].bitcast(F32), 1.0), row_ready)
                elif kind == "lower":
                    dve.wait_ge(tables_ready, 1)
                    emit(dve.tensor_copy(rot[DIM:P, :, 0, :], rot[DIM:P, :, 1, :]))
                elif kind == "ln":
                    b = step[1]
                    k = mini_norms[b]
                    mini_norms[b] += 1
                    dve.wait_ge(h_full[b], k + 1)
                    for t in range(TPB):
                        emit(dve.bn_stats(st[:, t, :], h[b][:, t, :]), hold=t == TPB - 1)
                    for t in range(TPB):
                        emit(dve.bn_aggr(mvs[b][:, t, :], st[:, t, :]), hold=t == TPB - 1)
                    emit(dve.tensor_scalar(var[b][:], mvs[b][:, :, 1], EPS, None, ALU.add), var_ready[b])
                elif kind == "scale":
                    b = step[1]
                    k = mini_norms[b] - 1
                    mean = mvs[b][:, :, 0:1].to_broadcast([P, TPB, DIM])
                    emit(dve.tensor_tensor(cen[:], h[b], mean, ALU.subtract))
                    dve.wait_ge(root_ready[b], k + 1)
                    src = cen[:].unsqueeze(2).to_broadcast([P, TPB, 2, DIM])
                    dst = lno[b].rearrange("p t (c d) -> p t c d", c=2)
                    by = root[b][:].unsqueeze(2).unsqueeze(3).to_broadcast([P, TPB, 2, DIM])
                    emit(dve.tensor_tensor(dst, src, by, ALU.mult), ln_ready[b])
                elif kind == "low":
                    b = step[1]
                    lows[b] += 1
                    dve.wait_ge(y_ready[b], 2 * lows[b] if lows[b] <= DEPTH else 2 * DEPTH + 1)
                    emit(dve.tensor_tensor(xs[b][DIM:P, :], ymini[b][DIM:P, :],
                                           xs[b][DIM:P, :].bitcast(F32), ALU.subtract), low_ready[b])
                elif kind == "scan":
                    _, b, l = step
                    y = ymini[b].rearrange("p (s t) -> p s t", s=SPB)
                    u = uscan[b].rearrange("p (s t) -> p s t", s=SPB)
                    turn = rot[:, l, 0, 0:SEQ].unsqueeze(1).to_broadcast([P, SPB, SEQ])
                    if l == 0:
                        dve.wait_ge(rad_ready, 1)
                    dve.wait_ge(y_ready[b], 2 * l + 1)
                    emit(dve.tensor_tensor(y, y, turn, ALU.mult))
                    for s in range(SPB):
                        emit(dve.tensor_tensor_scan(u[:, s, :], rad[:, l:l + 1].to_broadcast([P, SEQ]),
                                                    y[:, s, :], scan0[:, l:l + 1], ALU.mult, ALU.add),
                             hold=s == SPB - 1)
                    emit(dve.scalar_tensor_tensor(out=y, in0=u, scalar=col("scl", l), in1=turn,
                                                  op0=ALU.mult, op1=ALU.mult), z_ready[b])
                elif kind == "cast" and step[1:] not in ternary["act"]:
                    _, what, i = step
                    landed(dve, step[1:])
                    c0, c1 = chunk_range(what, i)
                    src = stage[:, slot(step[1:]), 0:c1 - c0]
                    if what in codes:
                        emit(dve.tensor_copy(codes[what][:, i, :], src), codes_ready["dve"])
                    elif what == "mask":
                        nb = D // MB
                        emit(dve.tensor_reduce(msum[:, i * nb:(i + 1) * nb],
                                               src.rearrange("p (a n) -> p a n", n=MB), AX.X, ALU.add),
                             masked)
                    else:
                        src = src.bitcast(F32)
                        if what == "V1":
                            wait_full(dve, ("up", 1, 2 * i + 1))
                        if what == "U2":
                            wait_full(dve, ("up", 1, FT - 1))
                        if what == "V2":
                            wait_full(dve, ("down", 1, TPB - 1))
                        if what == "w":
                            if i == 0:
                                wait_full(dve, ("wo", 1, TPB - 1))
                            dve.wait_ge(w_masked, i + 1)
                        hi = split[what][0]
                        emit(dve.tensor_copy(hi[:, c0:c1], src), part_hi)
                elif kind == "maskones":
                    wait_full(dve, step)
                    emit(dve.tensor_scalar(m01[:], bank_of(step)[:, 0:KT * D // MB], 0.0, None,
                                           ALU.is_gt), mask_on)
                elif kind == "up":
                    _, b, f = step
                    n = unit(b, f)
                    if n >= UNITS:
                        dve.wait_ge(hid_lo, n - UNITS + 1)
                    dve.wait_ge(silu_ready, n + 1)
                    wait_full(dve, step)
                    emit(dve.scalar_tensor_tensor(out=hid[:, n % UNITS, :], in0=bank_of(step)[:],
                                                  scalar=col("up_s", f), in1=silu[:, n % UNITS, :],
                                                  op0=ALU.mult, op1=ALU.mult), hid_ready)
                elif kind == "down" and step[3] == DPIECES - 1:
                    _, b, t, _ = step
                    n = b * TPB + t
                    wait_full(dve, ("down", b, t))
                    if n == 0:
                        dve.wait_ge(bc_in, 16)
                    if t == 0:
                        dve.wait_ge(x_biased, TPB * (b + 1))
                    emit(dve.tensor_tensor(tmp[:], bank_of(("down", b, t))[:], bc[:, DOWN_S, :],
                                           ALU.mult), down_read)
                    emit(dve.tensor_tensor(X[:, n, :], X[:, n, :], tmp[:], ALU.add))
                elif kind == "wo":
                    _, b, t = step
                    n = b * TPB + t
                    wait_full(dve, step)
                    dve.wait_ge(x_biased, TPB * (b + 1))
                    emit(dve.tensor_tensor(X[:, n, :], X[:, n, :], bank_of(step)[:], ALU.add), wo_added[b])
                elif kind == "u1":
                    dve.wait_ge(p_hi, step[1] + 1)
                    emit(dve.tensor_tensor(pl, bank_of(step)[:], ph.bitcast(F32), ALU.subtract), p_lo)
                elif kind == "hidden":
                    _, b, i = step
                    n = unit1(b, i)
                    K = rows_of(i)
                    key = ("hup", b, i)
                    dve.wait_ge(hid_lo, n - UNITS + 1)
                    dve.wait_ge(silu_ready, n + 1)
                    wait_full(dve, key)
                    emit(dve.scalar_tensor_tensor(out=hid[0:K, n % UNITS, :], in0=bank_of(key)[0:K, :],
                                                  scalar=col("fb_up", i)[0:K, :],
                                                  in1=silu[0:K, n % UNITS, :],
                                                  op0=ALU.add, op1=ALU.mult), hid_ready)
                elif kind == "zcopy":
                    dve.wait_ge(z_hi, step[1] + 1)
                    emit(dve.tensor_tensor(zl, banks[RING][:], zh.bitcast(F32), ALU.subtract), z_lo)
                elif kind == "out":
                    _, b, t = step
                    n = b * TPB + t
                    dve.wait_ge(y_biased, n + 1)
                    wait_full(dve, ("attn", b, t))
                    emit(dve.tensor_tensor(X[:, n, :], X[:, n, :], bank_of(("attn", b, t))[:],
                                           ALU.add), out_ready)

        @block.gpsimd
        def _(pool):
            done = [0]

            def link(ins):
                done[0] += 1
                ins.then_inc(pool_chain, 1)
                pool.wait_ge(pool_chain, done[0])

            link(pool.memset(powers[:, 0, :], -0.5))
            link(pool.memset(powers[:, 1, :], 0.5))
            rooted = [0] * NBLK + [0]

            def inverse_root(i, t=0, n=TPB):
                rooted[i] += 1
                pool.wait_ge(var_ready[i], rooted[i])
                pool.tensor_tensor(root[i][:, t:t + n], var[i][:, t:t + n], powers[:, 0, t:t + n],
                                   ALU.pow).then_inc(root_ready[i], 1)

            for step in order:
                kind = step[0]
                if kind == "seed":
                    re, im = col("re", 0, DEPTH), col("im", 0, DEPTH)
                    s2, size, inv, zero, re1, im1, c0, c1 = (pz[:, i, :] for i in range(8))
                    pool.wait_ge(prm_in, 16)
                    link(pool.tensor_tensor(s2, re, re, ALU.mult))
                    link(pool.tensor_tensor(c0, im, im, ALU.mult))
                    link(pool.tensor_tensor(s2, s2, c0, ALU.add))
                    pool.tensor_tensor(size, s2, powers[:, 1, :], ALU.pow).then_inc(size_ready, 1)
                elif kind == "grow" and step[1:] == (0, 0):
                    pool.wait_ge(size_ready, 1)
                    link(pool.tensor_scalar(zero, s2, 0.0, None, ALU.is_equal))
                    link(pool.tensor_tensor(re1, re, zero, ALU.add))
                    link(pool.tensor_tensor(zero, s2, zero, ALU.add))
                    link(pool.tensor_tensor(inv, zero, powers[:, 0, :], ALU.pow))
                    link(pool.tensor_scalar(im1, im, -1.0, None, ALU.mult))
                    link(pool.tensor_tensor(rot[:, :, 0, 1], re1, inv, ALU.mult))
                    link(pool.tensor_tensor(rot[:, :, 1, 1], im1, inv, ALU.mult))
                    link(pool.memset(rot[:, :, 0, 0:1], 1.0))
                    link(pool.memset(rot[:, :, 1, 0:1], 0.0))
                    link(pool.tensor_tensor(c0, rot[:, :, 0, 1], col("lc_p", 0, DEPTH), ALU.mult))
                    link(pool.tensor_scalar(c1, col("lc_q", 0, DEPTH), col("sign"), None, ALU.mult))
                    link(pool.tensor_tensor(c1, rot[:, :, 1, 1], c1, ALU.mult))
                    link(pool.tensor_tensor(scan0[:], c0, c1, ALU.add))
                if kind == "grow" and step[1] < POOL_GROWTHS:
                    if step[1:] == (POOL_GROWTHS - 1, 3):
                        growth(pool, *step[1:]).then_inc(tables_ready, 1)
                    else:
                        link(growth(pool, *step[1:]))
                elif kind == "root":
                    inverse_root(NBLK, *step[3:])
                elif kind == "ln":
                    inverse_root(step[1])
                elif kind == "xbias":
                    b = step[1]
                    pool.wait_ge(bc_in, 16)
                    for t in range(TPB):
                        n = b * TPB + t
                        pool.wait_ge(xn_ready, n + 1)
                        pool.tensor_tensor(X[:, n, :], X[:, n, :], bc[:, BOUT, :],
                                           ALU.add).then_inc(x_biased, 1)
                elif kind == "ybias":
                    n = step[1] * TPB + step[2]
                    if n == 0:
                        pool.wait_ge(bias_in, 16)
                        link(pool.tensor_tensor(bias[:, 0, :], bias[:, 0, :], bias[:, 1, :], ALU.add))
                    pool.wait_ge(xn_ready, NBLK * TPB + n + 1)
                    pool.tensor_tensor(X[:, n, :], X[:, n, :], bias[:, 0, :], ALU.add).then_inc(y_biased, 1)
                elif kind == "up":
                    n = unit(step[1], step[2])
                    pool.wait_ge(hid_hi, n + 1)
                    pool.tensor_tensor(hidl[:, n % FT, :], hid[:, n % UNITS, :], hidh[:, n % FT, :],
                                       ALU.subtract).then_inc(hid_lo, 1)
                elif kind == "hidden":
                    n = unit1(step[1], step[2])
                    K = rows_of(step[2])
                    pool.wait_ge(hid_hi, n + 1)
                    pool.tensor_tensor(actl[0:K, n % UNITS, :], hid[0:K, n % UNITS, :],
                                       acth[0:K, n % UNITS, :].bitcast(F32), ALU.subtract).then_inc(hid_lo, 1)
                elif kind == "wmask":
                    cast, nb = ("w", step[1]), D // MB
                    landed(pool, cast)
                    pool.wait_ge(mask_on, 1)
                    on = m01[:, cast[1] * nb:(cast[1] + 1) * nb].unsqueeze(2).to_broadcast([P, nb, MB])
                    blocks = stage[:, slot(cast), :].bitcast(F32).rearrange("p (a n) -> p a n", n=MB)
                    pool.tensor_tensor(blocks, blocks, on, ALU.mult).then_inc(w_masked, 1)
                elif kind == "cast" and step[1:] in general:
                    n = general.index(step[1:])
                    c0, c1 = chunk_range(*step[1:])
                    hi, lo = split[step[1]]
                    pool.wait_ge(part_hi, n + 1)
                    K = DIM if step[1] in ("W1", "Wout") else P
                    pool.tensor_tensor(lo[0:K, c0:c1], stage[0:K, slot(step[1:]), 0:c1 - c0].bitcast(F32),
                                       hi[0:K, c0:c1].bitcast(F32), ALU.subtract).then_inc(part_lo, 1)


def kernel(**inputs):
    import numpy as np
    import concourse.bacc as bacc
    from concourse.bass_utils import run_bass_kernel_spmd

    a = {k: np.asarray(v) for k, v in inputs.items()}
    A = {k[8:]: v for k, v in a.items() if k.startswith("L0_attn_")}
    tern = {k[7:]: v for k, v in a.items() if k.startswith("L0_ffn_")}
    low = {k[7:]: v for k, v in a.items() if k.startswith("L1_ffn_")}

    def tiles(m, n):
        return np.ascontiguousarray(m.reshape(n, P).T)

    def both(m):
        return np.concatenate([m.T, m.T])

    def inter(m):
        padded = np.zeros(IT * P, m.dtype)
        padded[:INTER] = m
        return tiles(padded, IT)

    eye = np.eye(DIM, dtype=np.float32)
    parts = {
        "ident": np.eye(P, dtype=np.float32),
        "blockones": np.kron(np.eye(P // MB), np.ones((MB, MB))).astype(np.float32),
        "twoeye": np.concatenate([eye, eye]),
        "sign": np.repeat(np.array([[1.0], [-1.0]], np.float32), DIM, axis=0),
        "gate_s": tiles(tern["gate_s"], FT), "up_s": tiles(tern["up_s"], FT),
        "ln1_w": both(A["ln1_w"]), "ln1_b": both(A["ln1_b"]),
        "re": both(A["phz_re"]), "im": both(A["phz_im"]),
        "lc_p": np.concatenate([A["lc_re"].T, A["lc_im"].T]),
        "lc_q": np.concatenate([A["lc_im"].T, A["lc_re"].T]),
        "scl": both(A["sc_lin"]), "ln2_w": both(A["ln2_w"]), "ln2_b": both(A["ln2_b"]),
        "lnl_w": both(A["lnl_w"][None]), "lnl_b": both(A["lnl_b"][None]),
        "b1": A["b1"].reshape(DEPTH * FH, P).T,
        "fb_gate": inter(low["b1"][:INTER]), "fb_up": inter(low["b1"][INTER:]),
        "win": A["Win"].T.reshape(KT, P, DIM).transpose(1, 0, 2).reshape(P, KT * DIM),
        "w2": A["W2"].reshape(DEPTH, DIM, FH, P).transpose(3, 0, 2, 1).reshape(P, -1),
    }
    u2 = np.zeros((IT * P, RANK), np.float32)
    u2[:INTER] = low["U2"]

    def codes_in(m):
        return m.reshape(FT, P, KT, P).transpose(0, 3, 2, 1).reshape(FT, P, D)

    arrays = {
        "x": a["L0_attn_x"].reshape(NTOK // P, P, D),
        "gate": codes_in(tern["gate_t"]), "up": codes_in(tern["up_t"]),
        "down": tern["down_t"].T.reshape(FT, P, D),
        "mask": a["L1_attn_mask"].T.reshape(KT, P, D),
        "weight": a["L1_attn_weight"].T.reshape(KT, P, D),
        "v1": low["V1"],
        "u2": u2.reshape(IT, P, RANK).transpose(1, 0, 2).reshape(P, IT * RANK),
        "u1": low["U1"].reshape(KT, P, RANK).transpose(1, 0, 2).reshape(P, KT * RANK),
        "v2": low["V2"],
        "params": np.concatenate([parts[n] for n, _ in EARLY], axis=1),
        "params2": np.concatenate([parts[n] for n, _ in LATE], axis=1),
        "wide64": np.tile(np.concatenate([A["W1"].transpose(2, 0, 1).reshape(DIM, DEPTH * DFF),
                                          A["Wout"].T], axis=1), (2, 1)),
        "rows": np.stack([tern["down_s"], A["bout"], a["L1_attn_bias"], low["b2"]]),
        "rows64": np.concatenate([A["b2"], A["bin"][None]]).reshape(1, -1),
    }
    nc = bacc.Bacc("TRN2", target_bir_lowering=False, num_devices=1)
    feeds, args = {}, []
    for name, value in arrays.items():
        value = np.ascontiguousarray(value)
        feeds[f"in_{name}"] = value
        args.append(nc.dram_tensor(f"in_{name}", value.shape, mybir.dt.from_np(value.dtype),
                                   kind="ExternalInput").ap())
    out = nc.dram_tensor("out_x", (NTOK // P, P, D), F32, kind="ExternalOutput").ap()
    two_layers(nc, *args, out)
    result = run_bass_kernel_spmd(nc, [feeds], core_ids=[0])
    return result.results[0]["out_x"].reshape(4, SEQ, D)
```
